# Optimizing a Trainium2 kernel written in Bass

```python
import numpy as np
import jax
import jax.numpy as jnp

def _softmax(x, axis=-1):
    return jax.nn.softmax(x, axis=axis)

def _gelu(x):
    return jax.nn.gelu(x, approximate=True)

def _silu(x):
    return jax.nn.silu(x)

def _sigmoid(x):
    return jax.nn.sigmoid(x)

def _layernorm(x, axis=-1, eps=1e-05):
    m = jnp.mean(x, axis=axis, keepdims=True)
    v = jnp.var(x, axis=axis, keepdims=True)
    return (x - m) / jnp.sqrt(v + eps)

def _scatter_add(tgt, idx, src, axis=0):
    return tgt.at[idx].add(src)

def _segment_sum(src, seg, n):
    return jax.ops.segment_sum(src, seg, n)
kernel_name = 'mk_adaln_d2_jaxref_r8_33217f'

def setup_inputs(seed: int=0):
    np.random.seed(seed)
    _w = jnp.asarray

    def _L0_attn_setup():
        import jax, jax.numpy as jnp
        import numpy as np
        import math
        BATCH = 4
        SEQ = 512
        EMBED = 128
        NUM_HEADS = 16
        HEAD_DIM = EMBED // NUM_HEADS
        WINDOW_SIZE = 128
        RADIUS = 2 * WINDOW_SIZE
        CHUNK = RADIUS
        key = jax.random.key(seed)
        ks = jax.random.split(key, 9)
        init = lambda k, shape: (0.02 * jax.random.normal(k, shape)).astype(jnp.float32)
        return {'hidden_states': jax.random.normal(ks[0], (BATCH, SEQ, EMBED), dtype=jnp.float32), 'wq': init(ks[1], (EMBED, EMBED)), 'bq': init(ks[2], (EMBED,)), 'wk': init(ks[3], (EMBED, EMBED)), 'bk': init(ks[4], (EMBED,)), 'wv': init(ks[5], (EMBED, EMBED)), 'bv': init(ks[6], (EMBED,)), 'wo': init(ks[7], (EMBED, EMBED)), 'bo': init(ks[8], (EMBED,))}
    _L0_attn_in = _L0_attn_setup()

    def _L0_ffn_setup():
        import jax, jax.numpy as jnp
        import numpy as np
        D, H, E, K, S = (128, 256, 8, 2, 1)
        B, L = (4, 256)
        key = jax.random.key(seed)
        ks = jax.random.split(key, 9)
        std = 0.02
        return {'x': jax.random.normal(ks[0], (B, L, D), dtype=jnp.float32), 'router_w': jax.random.normal(ks[1], (E, D), dtype=jnp.float32) * std, 'experts_bias': jnp.zeros((E,), dtype=jnp.float32), 'w1': jax.random.normal(ks[2], (E, D, H), dtype=jnp.float32) * std, 'w3': jax.random.normal(ks[3], (E, D, H), dtype=jnp.float32) * std, 'w2': jax.random.normal(ks[4], (E, H, D), dtype=jnp.float32) * std, 'sw1': jax.random.normal(ks[5], (S, D, H), dtype=jnp.float32) * std, 'sw3': jax.random.normal(ks[6], (S, D, H), dtype=jnp.float32) * std, 'sw2': jax.random.normal(ks[7], (S, H, D), dtype=jnp.float32) * std}
    _L0_ffn_in = _L0_ffn_setup()
    _L0_c = _w((lambda *s: np.random.randn(*s).astype(np.float32) * 0.05)(4, 128))
    _L0_wmod = _w((lambda *s: np.random.randn(*s).astype(np.float32) * 0.05)(128, 6 * 128) * 128 ** (-0.5))

    def _L1_attn_setup():
        import jax, jax.numpy as jnp
        import numpy as np
        B, L, C, H, W = (4, 512, 128, 16, 64)
        D = C // H
        STRIDE = W // 2

        def _local_attention(x, w_qkv, b_qkv, w_out, b_out):
            b, l, c = x.shape
            pad = -l % W
            x = jnp.pad(x, ((0, 0), (0, pad), (0, 0)))
            lp = l + pad
            qkv = (x @ w_qkv + b_qkv).reshape(b, lp, 3, H, D).transpose(2, 0, 3, 1, 4)
            q, k, v = (qkv[0], qkv[1], qkv[2])
            nw = (lp - W) // STRIDE + 1
            idx = jnp.arange(nw)[:, None] * STRIDE + jnp.arange(W)[None, :]
            qw = q[:, :, idx, :]
            kw = k[:, :, idx, :]
            vw = v[:, :, idx, :]
            scores = jnp.einsum('bhnqd,bhnkd->bhnqk', qw, kw) / jnp.sqrt(jnp.float32(D))
            probs = jax.nn.softmax(scores, axis=-1)
            ow = jnp.einsum('bhnqk,bhnkd->bhnqd', probs, vw)
            o = ow.transpose(0, 2, 3, 1, 4).reshape(b, nw * W, c)
            o = o @ w_out + b_out
            return o[:, :l, :]
        key = jax.random.key(seed)
        k0, k1, k2 = jax.random.split(key, 3)
        s = 0.02
        return {'x': jax.random.normal(k0, (B, L, C), jnp.float32), 'w_qkv': jax.random.normal(k1, (C, 3 * C), jnp.float32) * s, 'b_qkv': jnp.zeros((3 * C,), jnp.float32), 'w_out': jax.random.normal(k2, (C, C), jnp.float32) * s, 'b_out': jnp.zeros((C,), jnp.float32)}
    _L1_attn_in = _L1_attn_setup()

    def _L1_ffn_setup():
        import jax, jax.numpy as jnp
        import numpy as np
        NUM_EXPERTS = 8
        TOP_K = 2
        key = jax.random.key(seed)
        ks = jax.random.split(key, 5)
        B, L, E, H, N = (2, 256, 128, 256, NUM_EXPERTS)
        return {'x': jax.random.normal(ks[0], (B, L, E), dtype=jnp.float32), 'gate_kernel': jax.random.normal(ks[1], (E, N), dtype=jnp.float32) / np.sqrt(E), 'w0_kernel': jax.random.normal(ks[2], (N, E, H), dtype=jnp.float32) / np.sqrt(E), 'w1_kernel': jax.random.normal(ks[3], (N, E, H), dtype=jnp.float32) / np.sqrt(E), 'wo_kernel': jax.random.normal(ks[4], (N, H, E), dtype=jnp.float32) / np.sqrt(H)}
    _L1_ffn_in = _L1_ffn_setup()
    _L1_c = _w((lambda *s: np.random.randn(*s).astype(np.float32) * 0.05)(4, 128))
    _L1_wmod = _w((lambda *s: np.random.randn(*s).astype(np.float32) * 0.05)(128, 6 * 128) * 128 ** (-0.5))
    _d = {'L0_attn_hidden_states': _L0_attn_in['hidden_states'], 'L0_attn_wq': _L0_attn_in['wq'], 'L0_attn_bq': _L0_attn_in['bq'], 'L0_attn_wk': _L0_attn_in['wk'], 'L0_attn_bk': _L0_attn_in['bk'], 'L0_attn_wv': _L0_attn_in['wv'], 'L0_attn_bv': _L0_attn_in['bv'], 'L0_attn_wo': _L0_attn_in['wo'], 'L0_attn_bo': _L0_attn_in['bo'], 'L0_ffn_router_w': _L0_ffn_in['router_w'], 'L0_ffn_experts_bias': _L0_ffn_in['experts_bias'], 'L0_ffn_w1': _L0_ffn_in['w1'], 'L0_ffn_w3': _L0_ffn_in['w3'], 'L0_ffn_w2': _L0_ffn_in['w2'], 'L0_ffn_sw1': _L0_ffn_in['sw1'], 'L0_ffn_sw3': _L0_ffn_in['sw3'], 'L0_ffn_sw2': _L0_ffn_in['sw2'], 'L0_c': _L0_c, 'L0_wmod': _L0_wmod, 'L1_attn_w_qkv': _L1_attn_in['w_qkv'], 'L1_attn_b_qkv': _L1_attn_in['b_qkv'], 'L1_attn_w_out': _L1_attn_in['w_out'], 'L1_attn_b_out': _L1_attn_in['b_out'], 'L1_ffn_gate_kernel': _L1_ffn_in['gate_kernel'], 'L1_ffn_w0_kernel': _L1_ffn_in['w0_kernel'], 'L1_ffn_w1_kernel': _L1_ffn_in['w1_kernel'], 'L1_ffn_wo_kernel': _L1_ffn_in['wo_kernel'], 'L1_c': _L1_c, 'L1_wmod': _L1_wmod}
    _x0 = _d['L0_attn_hidden_states']
    _d['L0_attn_hidden_states'] = jax.random.normal(jax.random.fold_in(jax.random.key(seed), 1), (4, 512, 128), dtype=_x0.dtype)
    del _x0
    return _d

def reference(L0_attn_hidden_states, L0_attn_wq, L0_attn_bq, L0_attn_wk, L0_attn_bk, L0_attn_wv, L0_attn_bv, L0_attn_wo, L0_attn_bo, L0_ffn_router_w, L0_ffn_experts_bias, L0_ffn_w1, L0_ffn_w3, L0_ffn_w2, L0_ffn_sw1, L0_ffn_sw3, L0_ffn_sw2, L0_c, L0_wmod, L1_attn_w_qkv, L1_attn_b_qkv, L1_attn_w_out, L1_attn_b_out, L1_ffn_gate_kernel, L1_ffn_w0_kernel, L1_ffn_w1_kernel, L1_ffn_wo_kernel, L1_c, L1_wmod):

    def _L0_attn_ref(hidden_states, wq, bq, wk, bk, wv, bv, wo, bo):
        import jax, jax.numpy as jnp
        import numpy as np
        import math
        BATCH = 4
        SEQ = 512
        EMBED = 128
        NUM_HEADS = 16
        HEAD_DIM = EMBED // NUM_HEADS
        WINDOW_SIZE = 128
        RADIUS = 2 * WINDOW_SIZE
        CHUNK = RADIUS
        B, T, E = hidden_states.shape
        H, D = (NUM_HEADS, HEAD_DIM)
        c = CHUNK
        nC = T // c

        def proj(w, b):
            y = hidden_states @ w + b
            return y.reshape(B, T, H, D).transpose(0, 2, 1, 3)
        q = proj(wq, bq)
        k = proj(wk, bk)
        v = proj(wv, bv)
        scale = jnp.sqrt(jnp.asarray(D, dtype=q.dtype))
        kp = jnp.pad(k, ((0, 0), (0, 0), (c, c), (0, 0)))
        vp = jnp.pad(v, ((0, 0), (0, 0), (c, c), (0, 0)))
        idx = jnp.arange(nC)[:, None] * c + jnp.arange(3 * c)[None, :]
        kb = kp[:, :, idx, :]
        vb = vp[:, :, idx, :]
        qb = q.reshape(B, H, nC, c, D)
        scores = jnp.einsum('bhncd,bhnkd->bhnck', qb, kb) / scale
        qpos = (jnp.arange(nC) * c)[:, None] + jnp.arange(c)
        kpos = (jnp.arange(nC) * c)[:, None] - c + jnp.arange(3 * c)
        valid = (jnp.abs(qpos[:, :, None] - kpos[:, None, :]) <= RADIUS) & (kpos[:, None, :] >= 0) & (kpos[:, None, :] < T)
        scores = jnp.where(valid[None, None], scores, -jnp.inf)
        p = jax.nn.softmax(scores, axis=-1)
        o = jnp.einsum('bhnck,bhnkd->bhncd', p, vb)
        o = o.reshape(B, H, T, D).transpose(0, 2, 1, 3).reshape(B, T, E)
        return o @ wo + bo

    def _L0_ffn_ref(x, router_w, experts_bias, w1, w3, w2, sw1, sw3, sw2):
        import jax, jax.numpy as jnp
        import numpy as np
        D, H, E, K, S = (128, 256, 8, 2, 1)
        B, L = (4, 256)
        b, l, d = x.shape
        xf = x.reshape(-1, d)
        sg = jnp.einsum('td,sdh->tsh', xf, sw1)
        su = jnp.einsum('td,sdh->tsh', xf, sw3)
        shared_out = jnp.einsum('tsh,shd->td', jax.nn.silu(sg) * su, sw2)
        logits = xf @ router_w.T + experts_bias
        rw, sel = jax.lax.top_k(logits, K)
        rw = jax.nn.softmax(rw.astype(jnp.float32), axis=-1).astype(x.dtype)
        cw = (jax.nn.one_hot(sel, E, dtype=x.dtype) * rw[..., None]).sum(axis=1)
        g = jnp.einsum('td,edh->teh', xf, w1)
        u = jnp.einsum('td,edh->teh', xf, w3)
        eo = jax.nn.silu(g) * u
        moe_out = jnp.einsum('te,teh,ehd->td', cw, eo, w2)
        return (moe_out + shared_out).reshape(b, l, d)

    def _L1_attn_ref(x, w_qkv, b_qkv, w_out, b_out):
        import jax, jax.numpy as jnp
        import numpy as np
        B, L, C, H, W = (4, 512, 128, 16, 64)
        D = C // H
        STRIDE = W // 2

        def _local_attention(x, w_qkv, b_qkv, w_out, b_out):
            b, l, c = x.shape
            pad = -l % W
            x = jnp.pad(x, ((0, 0), (0, pad), (0, 0)))
            lp = l + pad
            qkv = (x @ w_qkv + b_qkv).reshape(b, lp, 3, H, D).transpose(2, 0, 3, 1, 4)
            q, k, v = (qkv[0], qkv[1], qkv[2])
            nw = (lp - W) // STRIDE + 1
            idx = jnp.arange(nw)[:, None] * STRIDE + jnp.arange(W)[None, :]
            qw = q[:, :, idx, :]
            kw = k[:, :, idx, :]
            vw = v[:, :, idx, :]
            scores = jnp.einsum('bhnqd,bhnkd->bhnqk', qw, kw) / jnp.sqrt(jnp.float32(D))
            probs = jax.nn.softmax(scores, axis=-1)
            ow = jnp.einsum('bhnqk,bhnkd->bhnqd', probs, vw)
            o = ow.transpose(0, 2, 3, 1, 4).reshape(b, nw * W, c)
            o = o @ w_out + b_out
            return o[:, :l, :]
        return _local_attention(x, w_qkv, b_qkv, w_out, b_out)

    def _L1_ffn_ref(x, gate_kernel, w0_kernel, w1_kernel, wo_kernel):
        import jax, jax.numpy as jnp
        import numpy as np
        NUM_EXPERTS = 8
        TOP_K = 2
        B, L, E = x.shape
        gate_logits = jnp.einsum('ble,en->bln', x, gate_kernel)
        top_k_weights, top_k_indices = jax.lax.top_k(gate_logits, TOP_K)
        softmax_probs = jax.nn.softmax(top_k_weights.astype(jnp.float32), axis=-1)
        weights = jnp.zeros_like(gate_logits)
        b_idx = jnp.arange(B)[:, None, None]
        l_idx = jnp.arange(L)[:, None]
        weights = weights.at[b_idx, l_idx, top_k_indices].set(softmax_probs)
        layer_w0 = jnp.einsum('ble,neh->blnh', x, w0_kernel)
        layer_w1 = jnp.einsum('ble,neh->blnh', x, w1_kernel)
        layer_mult = jax.nn.silu(layer_w0) * layer_w1
        intermediate = jnp.einsum('blnh,nhe->blne', layer_mult, wo_kernel)
        output = jnp.einsum('blne,bln->ble', intermediate, weights)
        return output
    x = L0_attn_hidden_states
    mod = (_silu(L0_c) @ L0_wmod).reshape(L0_c.shape[0], 6, 1, -1)
    sa, ca, ga, sb, cb, gb = (mod[:, 0], mod[:, 1], mod[:, 2], mod[:, 3], mod[:, 4], mod[:, 5])
    ga = (2 * (ga >= 0) - 1) * jnp.maximum(jnp.abs(ga), 0.25)
    gb = (2 * (gb >= 0) - 1) * jnp.maximum(jnp.abs(gb), 0.25)
    h = _layernorm(x, axis=-1) * (1 + ca) + sa
    x = x + ga * _L0_attn_ref(h, L0_attn_wq, L0_attn_bq, L0_attn_wk, L0_attn_bk, L0_attn_wv, L0_attn_bv, L0_attn_wo, L0_attn_bo)
    h = _layernorm(x, axis=-1) * (1 + cb) + sb
    x = x + gb * _L0_ffn_ref(h, L0_ffn_router_w, L0_ffn_experts_bias, L0_ffn_w1, L0_ffn_w3, L0_ffn_w2, L0_ffn_sw1, L0_ffn_sw3, L0_ffn_sw2)
    mod = (_silu(L1_c) @ L1_wmod).reshape(L1_c.shape[0], 6, 1, -1)
    sa, ca, ga, sb, cb, gb = (mod[:, 0], mod[:, 1], mod[:, 2], mod[:, 3], mod[:, 4], mod[:, 5])
    ga = (2 * (ga >= 0) - 1) * jnp.maximum(jnp.abs(ga), 0.25)
    gb = (2 * (gb >= 0) - 1) * jnp.maximum(jnp.abs(gb), 0.25)
    h = _layernorm(x, axis=-1) * (1 + ca) + sa
    x = x + ga * _L1_attn_ref(h, L1_attn_w_qkv, L1_attn_b_qkv, L1_attn_w_out, L1_attn_b_out)
    h = _layernorm(x, axis=-1) * (1 + cb) + sb
    x = x + gb * _L1_ffn_ref(h, L1_ffn_gate_kernel, L1_ffn_w0_kernel, L1_ffn_w1_kernel, L1_ffn_wo_kernel)
    return x

_drawn_inputs = setup_inputs


def setup_inputs(seed=0):
    import zlib

    import numpy as np

    out = dict(_drawn_inputs(seed))
    spreads = {'L0_ffn_experts_bias': (0.0, 0.8),
     'L1_attn_b_qkv': (0.0, 0.8),
     'L1_attn_b_out': (0.0, 0.301)}
    factors = {'L0_attn_wq': 8.0,
     'L0_attn_bq': 8.0,
     'L0_attn_wk': 8.0,
     'L0_attn_bk': 8.0,
     'L0_attn_wv': 8.0,
     'L0_attn_bv': 8.0,
     'L0_attn_wo': 8.0,
     'L0_attn_bo': 8.0,
     'L0_ffn_router_w': 8.0,
     'L0_ffn_w1': 8.0,
     'L0_ffn_w3': 8.0,
     'L0_ffn_w2': 8.0,
     'L0_ffn_sw1': 8.0,
     'L0_ffn_sw3': 8.0,
     'L0_ffn_sw2': 8.0,
     'L0_c': 6.761,
     'L0_wmod': 6.959,
     'L1_attn_w_qkv': 8.0,
     'L1_attn_w_out': 6.665}
    for name, (base, spread) in spreads.items():
        noise = np.random.default_rng([zlib.crc32(name.encode()), seed]).standard_normal(out[name].shape)
        drawn = base * np.exp(spread * noise) if base else spread * noise
        out[name] = jnp.asarray(drawn.astype(out[name].dtype))
    for name, factor in factors.items():
        out[name] = (out[name] * factor).astype(out[name].dtype)
    return out
```

```python
from contextlib import ExitStack

import concourse.bass as bass
from concourse import mybir

F32 = mybir.dt.float32
BF16 = mybir.dt.bfloat16
U32 = mybir.dt.uint32
ALU = mybir.AluOpType
ACT = mybir.ActivationFunctionType
AX = mybir.AxisListType

P = 128
B, SEQ, D = 4, 512, 128
LAYERS = 2
T = SEQ // P
HEADS, HD = 16, 8
PAIRS = HEADS // 2
E, HID = 8, 256
HC = HID // P
EXPERTS = [E + 1, E]
UNITS = [n * HC for n in EXPERTS]
WIN, STRIDE = 64, 32
NWIN = SEQ // WIN
EPS = 1e-5
GATE_MIN = 0.25
SCALE = float(HD) ** -0.5
MASKED = -1e30

PARTS = 3
SLOTS = 6
TOP = SLOTS * HD
COL = 32
GROUPS = HEADS // 4

KEY_TILES = [1, 2, 0, 3]
NEAR = {0: (0, 3), 1: (0, 4), 2: (0, 4), 3: (1, 4)}
CUT = {0: 2, 1: 3, 2: 0, 3: 1}


def adaln_two_layers(nc, x, cT, wmod, wq, wk, wv, wo, bq, bk, bv, bo, router, ebias, wup, wdn, out):
    with ExitStack() as ctx:
        def sb(name, shape, dt=F32):
            return ctx.enter_context(nc.sbuf_tensor(name, shape, dt))

        def ps(name, shape, dt=F32):
            return ctx.enter_context(nc.psum_tensor(name, shape, dt))

        def sem(name):
            return ctx.enter_context(nc.semaphore(name))

        wq_sb = [sb(f"wq{l}_sb", [P, D]) for l in range(LAYERS)]
        wk_sb = [sb(f"wk{l}_sb", [P, D]) for l in range(LAYERS)]
        wv_sb = [sb(f"wv{l}_sb", [P, D]) for l in range(LAYERS)]
        wo_sb = [sb(f"wo{l}_sb", [P, D]) for l in range(LAYERS)]
        bq_sb = [sb(f"bq{l}_sb", [P, 1]) for l in range(LAYERS)]
        bk_sb = [sb(f"bk{l}_sb", [P, 1]) for l in range(LAYERS)]
        bv_sb = [sb(f"bv{l}_sb", [P, D]) for l in range(LAYERS)]
        bo_sb = [sb(f"bo{l}_sb", [P, D]) for l in range(LAYERS)]
        router_sb = [sb(f"router{l}_sb", [P, E]) for l in range(LAYERS)]
        ebias_sb = sb("ebias_sb", [P, E])
        wup_sb = [sb(f"wup{l}_sb", [P, EXPERTS[l], 2, HID]) for l in range(LAYERS)]
        wdn_sb = [sb(f"wdn{l}_sb", [P, EXPERTS[l], HC, D]) for l in range(LAYERS)]
        wmod_sb = sb("wmod_sb", [P, LAYERS, 6, D])
        cT_sb = sb("cT_sb", [P, LAYERS, B])
        c_act = sb("c_act", [P, LAYERS, B])
        c_rows = sb("c_rows", [P, LAYERS, B, P])
        modT = sb("modT", [P, LAYERS, 2, 2, B])
        gate = sb("gate", [P, LAYERS, B, 2, D])
        gate_sign = sb("gate_sign", [P, 2, D])
        gate_size = sb("gate_size", [P, 2, D])
        gate_bo = sb("gate_bo", [P, LAYERS, B, D])
        ident = sb("ident", [P, P])
        ident_b = sb("ident_b", [P, P], BF16)
        cut_late = sb("cut_late", [P, P], BF16)
        cut_early = sb("cut_early", [P, P], BF16)
        minus_half = sb("minus_half", [P, T])
        iota_i = sb("iota_i", [P, E], mybir.dt.int32)
        iota_f = sb("iota_f", [P, E])
        ones_b = sb("ones_b", [PARTS, PAIRS * SEQ], BF16)

        X = sb("X", [P, T, D])
        modb = sb("modb", [P, LAYERS, 2, 2])
        stats = sb("stats", [P, T, 6])
        mv = sb("mv", [P, T, 2])
        var_eps = sb("var_eps", [P, T])
        rstd = sb("rstd", [P, T])
        xh = sb("xh", [P, T, D])
        hT = sb("hT", [P, SEQ])
        qf = sb("qf", [P, SEQ])
        kf = sb("kf", [P, SEQ])
        q_rest = sb("q_rest", [P, SEQ])
        k_rest = sb("k_rest", [P, SEQ])
        q_parts = sb("q_parts", [P, PARTS, SEQ], BF16)
        k_parts = sb("k_parts", [P, PARTS, SEQ], BF16)
        qs = sb("qs", [P, PAIRS, SEQ], BF16)
        ks = sb("ks", [P, 2, PAIRS, SEQ], BF16)
        V = sb("V", [P, T, HEADS, COL])
        M = sb("M", [P, T, PAIRS, 2])
        m_rest = sb("m_rest", [P, T, PAIRS, 2])
        m_parts = sb("m_parts", [P, T, 2, PARTS, PAIRS], BF16)
        mT = sb("mT", [2 * PARTS * PAIRS, SEQ], BF16)
        prob = sb("prob", [P, 2, 4, SEQ])
        win_prob = sb("win_prob", [P, 2, HEADS, P])
        oT = sb("oT", [P, GROUPS, SEQ])
        rden = sb("rden", [P, T, HEADS])
        att = sb("att", [P, T, D])
        attT = sb("attT", [P, SEQ])
        gated = sb("gated", [P, T, D])
        logit = sb("logit", [P, T, E])
        top = sb("top", [P, T, E])
        top_i = sb("top_i", [P, T, E], U32)
        top_if = sb("top_if", [P, T, 2])
        gap = sb("gap", [P, T])
        gap_e = sb("gap_e", [P, T])
        gap_s = sb("gap_s", [P, T])
        w_top = sb("w_top", [P, 2, T])
        pick = sb("pick", [P, 2, T, E])
        cw = sb("cw", [P, T, E])
        silu = sb("silu", [P, 2, SEQ])
        hid = sb("hid", [P, 2, SEQ])
        acc = sb("acc", [P, T, D])

        wide = [ps(f"wide{i}", [P, 2, SEQ]) for i in range(2)]
        bank = [ps(f"bank{i}", [P, SEQ]) for i in range(4)]

        q_dram = nc.dram_tensor("q_dram", (2, PARTS * HD + PARTS, PAIRS, SEQ), BF16, kind="Internal").ap()
        k_dram = nc.dram_tensor("k_dram", (2, PARTS * HD, PAIRS, SEQ), BF16, kind="Internal").ap()
        m_dram = nc.dram_tensor("m_dram", (2, PARTS, PAIRS, SEQ), BF16, kind="Internal").ap()

        s_w = sem("weights_loaded")
        s_wb = sem("expert_weights_loaded")
        s_const = sem("constants_made")
        s_identb = sem("vector_constants_made")
        s_ones = sem("ones_placed")
        s_cact = sem("conditioning_activated")
        s_crow = sem("conditioning_rows")
        s_modps = sem("modulation_in_psum")
        s_mod = sem("modulation_copied")
        s_gps = sem("gates_in_psum")
        s_gate = sem("gates_made")
        s_x = sem("x_loaded")
        s_modb = sem("modulation_of_b")
        s_stat = sem("norm_stats")
        s_aggr = sem("norm_mean_var")
        s_var = sem("norm_var_eps")
        s_rstd = sem("norm_rstd")
        s_xh = sem("normalised")
        s_xT = sem("normalised_T_psum")
        s_hT = sem("hT_ready")
        s_qps = sem("q_psum")
        s_kps = sem("k_psum")
        s_vps = sem("v_psum")
        s_qf = sem("q_copied")
        s_kf = sem("k_copied")
        s_qsp = sem("q_split")
        s_ksp = sem("k_split")
        s_v = sem("v_copied")
        s_qw = sem("q_parts_stored")
        s_kw = sem("k_parts_stored")
        s_qs = sem("q_stack_loaded")
        s_ks = sem("k_stack_loaded")
        s_S = sem("scores_for_max")
        s_mx = sem("max_taken")
        s_msp = sem("max_split")
        s_mTp = sem("max_T_psum")
        s_mT = sem("max_T_copied")
        s_mw = sem("max_stored")
        s_mr = sem("max_stacked")
        s_T = sem("scores_for_exp")
        s_ex = sem("exp_done")
        s_cut = sem("band_cut")
        s_pv = sem("pv_done")
        s_oT = sem("oT_copied")
        s_o = sem("o_psum")
        s_rden = sem("denominator_inverse")
        s_att = sem("attention_normed")
        s_aTp = sem("attention_T_psum")
        s_aT = sem("attention_T_copied")
        s_pr = sem("projected")
        s_gbo = sem("bias_added")
        s_gx = sem("gated_attention")
        s_xa = sem("x_after_attention")
        s_lg = sem("logits_psum")
        s_lb = sem("logits_ready")
        s_m8 = sem("top_values")
        s_ix = sem("top_indices")
        s_gap = sem("top_gap")
        s_ge = sem("top_gap_exp")
        s_w12 = sem("top_weights")
        s_pick = sem("picked")
        s_cw = sem("expert_weights")
        s_gu = sem("up_psum")
        s_sg = sem("silu_done")
        s_hid = sem("hidden_ready")
        s_dn = sem("down_psum")
        s_acc = sem("expert_added")
        s_gy = sem("gated_experts")
        s_xe = sem("x_after_experts")
        s_out = sem("stored")

        N_MAX = [T * PAIRS, T]
        N_EXP = [GROUPS * T * 2, T]
        S0, S1 = 0, N_MAX[0]
        N_S = sum(N_MAX)
        N_T = sum(N_EXP)
        N_EX = N_EXP[0] + 2 * T
        N_PV = GROUPS * T + T
        N_UNIT = sum(UNITS)
        N_DN = sum(EXPERTS)
        N_SMALL = 16 * (2 * LAYERS + 9 * LAYERS + 1)
        GATES = LAYERS * B
        N_CONST = 9

        def windows(tile):
            first = tile[:, 0:WIN]
            return bass.AP(first.tensor, first.offset, [list(first.ap[0]), [STRIDE, NWIN], [1, WIN]])

        block = ctx.enter_context(nc.Block())

        @block.sync
        def _(sp):
            for l in range(LAYERS):
                sp.dma_start(cT_sb[:, l, :], cT[l]).then_inc(s_w, 16)
                sp.dma_start(wmod_sb[:, l, :, :].rearrange("p j f -> p (j f)"), wmod[l]).then_inc(s_w, 16)
            for l in range(LAYERS):
                for dst, src in ((wq_sb, wq), (wk_sb, wk), (wv_sb, wv), (wo_sb, wo), (bq_sb, bq),
                                 (bk_sb, bk), (router_sb, router)):
                    sp.dma_start(dst[l][:], src[l]).then_inc(s_w, 16)
                for dst, src in ((bv_sb, bv), (bo_sb, bo)):
                    sp.dma_start(dst[l][:], src[l].partition_broadcast(P)).then_inc(s_w, 16)
            sp.dma_start(ebias_sb[:], ebias.partition_broadcast(P)).then_inc(s_w, 16)
            sp.wait_ge(s_const, 1)
            sp.wait_ge(s_identb, 1)
            for half in range(2):
                r = 64 * half + TOP
                sp.dma_start(ks[r:r + PARTS, half, :, :].rearrange("p a s -> p (a s)"),
                             ones_b[:]).then_inc(s_ones, 16)
                sp.dma_start(q_dram[half, PARTS * HD:, :, :].rearrange("p a s -> p (a s)"),
                             qs[0:PARTS, :, :].rearrange("p a s -> p (a s)")).then_inc(s_ones, 16)
            with sp.Fori(0, B) as b:
                sp.dma_start(X[:], x[b].rearrange("(t p) d -> p t d", p=P)).then_inc(s_x, 16)
                for l in range(LAYERS):
                    u = b * 2 + l
                    sp.wait_ge(s_qsp, u * 4 + 4)
                    for half in range(2):
                        sp.dma_start(q_dram[half, 0:PARTS * HD, :, :].rearrange("(c d) a s -> (d a) c s", d=HD),
                                     q_parts[64 * half:64 * half + 64, :, :]).then_inc(s_qw, 16)
                    sp.wait_ge(s_ksp, u * 4 + 4)
                    for half in range(2):
                        sp.dma_start(k_dram[half].rearrange("(c d) a s -> (d a) c s", d=HD),
                                     k_parts[64 * half:64 * half + 64, :, :]).then_inc(s_kw, 16)
                    sp.wait_ge(s_qw, u * 32 + 32)
                    for half in range(2):
                        r = 64 * half
                        q_h = q_dram[half].rearrange("r a s -> r (a s)")
                        qs_h = qs[:, :, :].rearrange("p a s -> p (a s)")
                        sp.dma_start(qs_h[r:r + 24, :], q_h[0:24, :]).then_inc(s_qs, 16)
                        sp.dma_start(qs_h[r + 24:r + 32, :], q_h[0:8, :]).then_inc(s_qs, 16)
                        sp.dma_start(qs_h[r + 32:r + 40, :], q_h[16:24, :]).then_inc(s_qs, 16)
                        sp.dma_start(qs_h[r + 40:r + 51, :], q_h[16:27, :]).then_inc(s_qs, 16)
                    sp.wait_ge(s_kw, u * 32 + 32)
                    for half in range(2):
                        r = 64 * half
                        k_h = k_dram[half].rearrange("r a s -> r (a s)")
                        ks_h = ks[:, half, :, :].rearrange("p a s -> p (a s)")
                        sp.dma_start(ks_h[r:r + 16, :], k_h[0:16, :]).then_inc(s_ks, 16)
                        sp.dma_start(ks_h[r + 16:r + 32, :], k_h[0:16, :]).then_inc(s_ks, 16)
                        sp.dma_start(ks_h[r + 32:r + 48, :], k_h[8:24, :]).then_inc(s_ks, 16)
                    sp.wait_ge(s_mT, u + 1)
                    sp.dma_start(m_dram.rearrange("h c a s -> (h c a) s"), mT[:]).then_inc(s_mw, 16)
                    sp.wait_ge(s_mw, u * 16 + 16)
                    for half in range(2):
                        r = 64 * half + TOP
                        sp.dma_start(qs[r:r + PARTS, :, :].rearrange("p a s -> p (a s)"),
                                     m_dram[half].rearrange("c a s -> c (a s)")).then_inc(s_mr, 16)
                sp.wait_ge(s_xe, b * 2 + 2)
                sp.dma_start(out[b].rearrange("(t p) d -> p t d", p=P), X[:]).then_inc(s_out, 16)
                need = sp.to_reg(b * 16 + 16)
                sp.wait_ge(s_const, N_CONST)
                sp.wait_ge(s_out, need)

        @block.gpsimd
        def _(pool):
            for l in range(LAYERS):
                pool.dma_start(wup_sb[l][:], wup[l].rearrange("p (e g h) -> p e g h", g=2, h=HID)).then_inc(s_wb, 16)
                pool.dma_start(wdn_sb[l][:], wdn[l].rearrange("p (e c d) -> p e c d", c=HC, d=D)).then_inc(s_wb, 16)
            pool.memset(ones_b[:], 1.0).then_inc(s_const, 1)
            pool.memset(ident[:], 0.0).then_inc(s_const, 1)
            pool.memset(cut_late[:], 0.0).then_inc(s_const, 1)
            pool.memset(cut_early[:], 0.0).then_inc(s_const, 1)
            pool.memset(minus_half[:], -0.5).then_inc(s_const, 1)
            pool.wait_ge(s_const, 5)
            pool.affine_select(out=ident[:], in_=ident[:], compare_op=ALU.not_equal, fill=1.0, base=0,
                               pattern=[[-1, P]], channel_multiplier=1).then_inc(s_const, 1)
            pool.affine_select(out=cut_late[:], in_=cut_late[:], compare_op=ALU.is_ge, fill=MASKED, base=0,
                               pattern=[[-1, P]], channel_multiplier=1).then_inc(s_const, 1)
            pool.affine_select(out=cut_early[:], in_=cut_early[:], compare_op=ALU.is_ge, fill=MASKED, base=0,
                               pattern=[[1, P]], channel_multiplier=-1).then_inc(s_const, 1)
            pool.iota(iota_i[:], pattern=[[1, E]], base=0, channel_multiplier=0).then_inc(s_const, 1)

            def norm(b, l, w):
                z = b * 4 + (2 * l + w)
                need = pool.to_reg(z * 4 + 4)
                pool.wait_ge(s_const, N_CONST)
                pool.wait_ge(s_aggr, need)
                pool.tensor_scalar(var_eps[:], mv[:, :, 1], EPS, None, ALU.add).then_inc(s_var, 1)
                pool.wait_ge(s_var, z + 1)
                pool.tensor_tensor(rstd[:], var_eps[:], minus_half[:], ALU.pow).then_inc(s_rstd, 1)

            def split_k(b, l):
                u = b * 2 + l
                need = pool.to_reg(u + 1)
                pool.wait_ge(s_const, N_CONST)
                pool.wait_ge(s_kf, need)
                pool.tensor_copy(k_parts[:, 0, :], kf[:]).then_inc(s_ksp, 1)
                pool.wait_ge(s_ksp, u * 4 + 1)
                pool.tensor_tensor(k_rest[:], kf[:], k_parts[:, 0, :], ALU.subtract).then_inc(s_ksp, 1)
                need = pool.to_reg(u * 4 + 2)
                pool.wait_ge(s_const, N_CONST)
                pool.wait_ge(s_ksp, need)
                pool.tensor_copy(k_parts[:, 1, :], k_rest[:]).then_inc(s_ksp, 1)
                pool.wait_ge(s_ksp, u * 4 + 3)
                pool.tensor_tensor(k_parts[:, 2, :], k_rest[:], k_parts[:, 1, :], ALU.subtract).then_inc(s_ksp, 1)

            def add_bias(b, l):
                u = b * 2 + l
                pool.wait_ge(s_xh, u * 8 + 4)
                pool.wait_ge(s_gate, 5 * GATES)
                bias = gate_bo[:, l, bass.ds(b, 1), :].to_broadcast([P, T, D])
                pool.tensor_tensor(X[:], X[:], bias, ALU.add).then_inc(s_gbo, 1)

            with pool.Fori(0, B) as b:
                norm(b, 0, 0)
                split_k(b, 0)
                add_bias(b, 0)
                for g in range(GROUPS):
                    for i, kt in enumerate(KEY_TILES):
                        n = g * T + i
                        need = pool.to_reg(b * N_EX + (2 * n + 2))
                        pool.wait_ge(s_const, N_CONST)
                        pool.wait_ge(s_ex, need)
                        cut = prob[:, n % 2, :, P * CUT[kt]:P * CUT[kt] + P]
                        sign = 1 if CUT[kt] > kt else -1
                        pool.affine_select(out=cut, in_=cut, compare_op=ALU.is_ge, fill=0.0, base=0,
                                           pattern=[[0, 4], [-sign, P]], channel_multiplier=sign
                                           ).then_inc(s_cut, 1)
                norm(b, 0, 1)
                norm(b, 1, 0)
                split_k(b, 1)
                add_bias(b, 1)
                norm(b, 1, 1)

        @block.scalar
        def _(act):
            act.wait_ge(s_w, N_SMALL)
            act.activation(c_act[:], cT_sb[:], ACT.Silu).then_inc(s_cact, 1)

            def shift_scale(b, l, w):
                z = b * 4 + (2 * l + w)
                act.wait_ge(s_xT, z + 1)
                act.wait_ge(s_modb, b + 1)
                if (l, w) == (1, 0):
                    dst, src = hT[:].rearrange("p (n s) -> p n s", s=WIN), windows(bank[0])
                else:
                    dst, src = hT[:], bank[0][:]
                act.activation(dst, src, ACT.Identity, bias=modb[:, l, w, 0:1],
                               scale=modb[:, l, w, 1:2]).then_inc(s_hT, 1)

            def copy_qk(b, l):
                u = b * 2 + l
                act.wait_ge(s_qps, u + 1)
                act.activation(qf[:], bank[1][:], ACT.Identity, bias=bq_sb[l][:]).then_inc(s_qf, 1)
                act.wait_ge(s_kps, u + 1)
                act.activation(kf[:], bank[2][:], ACT.Identity, bias=bk_sb[l][:]).then_inc(s_kf, 1)

            def copy_attT(b, l):
                u = b * 2 + l
                act.wait_ge(s_aTp, u + 1)
                act.activation(attT[:], bank[0][:], ACT.Identity).then_inc(s_aT, 1)

            def experts(b, l):
                u = b * 2 + l
                act.wait_ge(s_gap, u * 2 + 1)
                act.activation(gap_e[:], gap[:], ACT.Exp).then_inc(s_ge, 1)
                for i in range(UNITS[l]):
                    n = UNITS[0] * l + i
                    act.wait_ge(s_gu, b * N_UNIT + (n + 1))
                    if i >= 2:
                        act.wait_ge(s_hid, b * N_UNIT + (n - 1))
                    act.activation(silu[:, i % 2, :], wide[i % 2][:, 0, :], ACT.Silu).then_inc(s_sg, 1)

            with act.Fori(0, B) as b:
                shift_scale(b, 0, 0)
                copy_qk(b, 0)
                for g in range(GROUPS):
                    for i, kt in enumerate(KEY_TILES):
                        n = g * T + i
                        for two in range(2):
                            act.wait_ge(s_T, b * N_T + (2 * n + two + 1))
                            if n >= 2:
                                act.wait_ge(s_pv, b * N_PV + (n - 1))
                            a, z = P * NEAR[kt][0], P * NEAR[kt][1]
                            act.activation(prob[:, n % 2, 2 * two:2 * two + 2, a:z], wide[two][:, :, a:z],
                                           ACT.Exp, scale=SCALE).then_inc(s_ex, 1)
                copy_attT(b, 0)
                shift_scale(b, 0, 1)
                experts(b, 0)
                shift_scale(b, 1, 0)
                copy_qk(b, 1)
                act.wait_ge(s_identb, 2)
                for t in range(T):
                    act.wait_ge(s_T, b * N_T + (N_EXP[0] + t + 1))
                    if t >= 2:
                        act.wait_ge(s_pv, b * N_PV + (GROUPS * T + t - 1))
                    for w in range(2):
                        r = WIN * w
                        src = wide[t % 2][r:r + WIN, :, :].rearrange("p a (h s) -> p (a h) s", s=WIN)
                        act.activation(win_prob[r:r + WIN, t % 2, :, r:r + WIN], src, ACT.Exp,
                                       scale=SCALE).then_inc(s_ex, 1)
                copy_attT(b, 1)
                shift_scale(b, 1, 1)
                experts(b, 1)

        @block.vector
        def _(dve):
            dve.memset(qs[:].rearrange("p a s -> p (a s)").bitcast(U32), 0)
            dve.memset(ks[:].rearrange("p c a s -> p (c a s)").bitcast(U32), 0).then_inc(s_identb, 1)
            dve.memset(win_prob[:], 0.0)
            dve.memset(V[:], 0.0).then_inc(s_crow, 1)
            dve.wait_ge(s_crow, 1)
            dve.memset(V[:, :, :, HD:HD + 1], 1.0)
            dve.wait_ge(s_const, N_CONST)
            dve.tensor_copy(iota_f[:], iota_i[:])
            dve.tensor_copy(ident_b[:], ident[:]).then_inc(s_identb, 1)
            dve.wait_ge(s_cact, 1)
            dve.tensor_copy(c_rows[:], c_act[:].unsqueeze(3).to_broadcast([P, LAYERS, B, P])).then_inc(s_crow, 1)
            dve.wait_ge(s_modps, 1)
            mod_ps = bank[0][:, 0:LAYERS * 4 * B].rearrange("p (l w k b) -> p l w k b", l=LAYERS, w=2, k=2)
            for l in range(LAYERS):
                for w in range(2):
                    dve.tensor_copy(modT[:, l, w, 0, :], mod_ps[:, l, w, 0, :]).then_inc(s_mod, 1)
                    dve.tensor_scalar(modT[:, l, w, 1, :], mod_ps[:, l, w, 1, :], 1.0, None,
                                      ALU.add).then_inc(s_mod, 1)
            for i in range(GATES):
                l, b = i // B, i % B
                g_ps = bank[1 + i % 2][:, 0:2 * D].rearrange("p (w d) -> p w d", w=2)
                dve.wait_ge(s_gps, i + 1)
                if i:
                    dve.wait_ge(s_gate, 5 * i)
                dve.tensor_scalar(gate_sign[:], g_ps, 0.0, 0.5, ALU.is_ge, ALU.subtract).then_inc(s_gate, 1)
                dve.tensor_scalar(gate_size[:], g_ps, -1.0, GATE_MIN, ALU.mult, ALU.max).then_inc(s_gate, 1)
                dve.wait_ge(s_gate, 5 * i + 2)
                dve.tensor_tensor(gate_size[:], g_ps, gate_size[:], ALU.max).then_inc(s_gate, 1)
                dve.wait_ge(s_gate, 5 * i + 3)
                dve.scalar_tensor_tensor(out=gate[:, l, b, :, :], in0=gate_size[:], scalar=2.0, in1=gate_sign[:],
                                         op0=ALU.mult, op1=ALU.mult).then_inc(s_gate, 1)
                dve.wait_ge(s_gate, 5 * i + 4)
                dve.tensor_tensor(gate_bo[:, l, b, :], gate[:, l, b, 0, :], bo_sb[l][:], ALU.mult).then_inc(s_gate, 1)

            def norm(b, l, w):
                z = b * 4 + (2 * l + w)
                for t in range(T):
                    dve.bn_stats(stats[:, t, :], X[:, t, :]).then_inc(s_stat, 1)
                for t in range(T):
                    need = dve.to_reg(z * 4 + (t + 1))
                    dve.wait_ge(s_const, N_CONST)
                    dve.wait_ge(s_stat, need)
                    dve.bn_aggr(mv[:, t, :], stats[:, t, :]).then_inc(s_aggr, 1)
                dve.wait_ge(s_rstd, z + 1)
                for t in range(T):
                    dve.tensor_scalar(xh[:, t, :], X[:, t, :], mv[:, t, 0:1], rstd[:, t:t + 1],
                                      ALU.subtract, ALU.mult).then_inc(s_xh, 1)

            def split_q(b, l):
                u = b * 2 + l
                dve.wait_ge(s_qf, u + 1)
                dve.tensor_copy(q_parts[:, 2, :], qf[:]).then_inc(s_qsp, 1)
                dve.wait_ge(s_qsp, u * 4 + 1)
                dve.tensor_tensor(q_rest[:], qf[:], q_parts[:, 2, :], ALU.subtract).then_inc(s_qsp, 1)
                dve.wait_ge(s_qsp, u * 4 + 2)
                dve.tensor_copy(q_parts[:, 0, :], q_rest[:]).then_inc(s_qsp, 1)
                dve.wait_ge(s_qsp, u * 4 + 3)
                dve.tensor_tensor(q_parts[:, 1, :], q_rest[:], q_parts[:, 0, :], ALU.subtract).then_inc(s_qsp, 1)
                dve.wait_ge(s_vps, u + 1)
                for t in range(T):
                    v = dve.tensor_tensor(V[:, t, :, 0:HD],
                                          bank[3][:, P * t:P * t + P].rearrange("p (h d) -> p h d", d=HD),
                                          bv_sb[l][:].rearrange("p (h d) -> p h d", d=HD), ALU.add)
                v.then_inc(s_v, 1)

            def split_max(b, l):
                u = b * 2 + l
                m = M[:].rearrange("p t a h -> p t h a")
                rest = m_rest[:].rearrange("p t a h -> p t h a")
                for t in range(T):
                    dve.tensor_scalar(m_parts[:, t, :, 0, :], m[:, t], -1.0, None, ALU.mult)
                    last = dve.tensor_scalar(rest[:, t], m[:, t], -1.0, None, ALU.mult)
                last.then_inc(s_msp, 1)
                dve.wait_ge(s_msp, u * 4 + 1)
                for t in range(T):
                    last = dve.tensor_tensor(rest[:, t], rest[:, t], m_parts[:, t, :, 0, :], ALU.subtract)
                last.then_inc(s_msp, 1)
                dve.wait_ge(s_msp, u * 4 + 2)
                for t in range(T):
                    last = dve.tensor_copy(m_parts[:, t, :, 1, :], rest[:, t])
                last.then_inc(s_msp, 1)
                dve.wait_ge(s_msp, u * 4 + 3)
                for t in range(T):
                    last = dve.tensor_tensor(m_parts[:, t, :, 2, :], rest[:, t], m_parts[:, t, :, 1, :],
                                             ALU.subtract)
                last.then_inc(s_msp, 1)
                dve.wait_ge(s_mTp, u + 1)
                dve.tensor_copy(mT[:], bank[0][:].bitcast(BF16)[0:2 * PARTS * PAIRS, 0:SEQ]).then_inc(s_mT, 1)

            def finish_attention(b, l):
                u = b * 2 + l
                for t in range(T):
                    o = wide[t // 2][:, t % 2, :].rearrange("p (h c) -> p h c", c=COL)
                    dve.wait_ge(s_o, u * 4 + (t + 1))
                    dve.reciprocal(rden[:, t, :], o[:, :, HD]).then_inc(s_rden, 1)
                    dve.wait_ge(s_rden, u * 4 + (t + 1))
                    dve.tensor_tensor(att[:, t, :].rearrange("p (h d) -> p h d", d=HD), o[:, :, 0:HD],
                                      rden[:, t, :].unsqueeze(2).to_broadcast([P, HEADS, HD]),
                                      ALU.mult).then_inc(s_att, 1)
                dve.wait_ge(s_pr, u + 1)
                ga = gate[:, l, bass.ds(b, 1), 0, :].to_broadcast([P, T, D])
                dve.tensor_tensor(gated[:], bank[1][:].rearrange("p (t d) -> p t d", t=T), ga,
                                  ALU.mult).then_inc(s_gx, 1)
                dve.wait_ge(s_gx, u + 1)
                dve.wait_ge(s_gbo, u + 1)
                dve.tensor_tensor(X[:], X[:], gated[:], ALU.add).then_inc(s_xa, 1)
                dve.wait_ge(s_xa, u + 1)

            def route(b, l):
                u = b * 2 + l
                dve.wait_ge(s_lg, u + 1)
                lg = bank[2][:, 0:T * E].rearrange("p (t e) -> p t e", e=E)
                if l == 0:
                    dve.tensor_tensor(logit[:], lg, ebias_sb[:].unsqueeze(1).to_broadcast([P, T, E]),
                                      ALU.add).then_inc(s_lb, 1)
                else:
                    dve.tensor_copy(logit[:], lg).then_inc(s_lb, 1)
                need = dve.to_reg(u + 1)
                dve.wait_ge(s_const, N_CONST)
                dve.wait_ge(s_lb, need)
                for t in range(T):
                    dve.max(top[:, t, :], logit[:, t, :]).then_inc(s_m8, 1)
                dve.wait_ge(s_m8, u * 4 + 4)
                dve.tensor_tensor(gap[:], top[:, :, 1], top[:, :, 0], ALU.subtract).then_inc(s_gap, 1)
                for t in range(T):
                    dve.max_index(top_i[:, t, :], top[:, t, :], logit[:, t, :]).then_inc(s_ix, 1)
                dve.wait_ge(s_ix, u * 4 + 4)
                dve.tensor_copy(top_if[:], top_i[:, :, 0:2]).then_inc(s_gap, 1)
                dve.wait_ge(s_ge, u + 1)
                dve.tensor_scalar(gap_s[:], gap_e[:], 1.0, None, ALU.add).then_inc(s_w12, 1)
                dve.wait_ge(s_w12, u * 3 + 1)
                dve.reciprocal(w_top[:, 0, :], gap_s[:]).then_inc(s_w12, 1)
                dve.wait_ge(s_w12, u * 3 + 2)
                dve.tensor_tensor(w_top[:, 1, :], w_top[:, 0, :], gap_e[:], ALU.mult).then_inc(s_w12, 1)
                dve.wait_ge(s_gap, u * 2 + 2)
                dve.wait_ge(s_w12, u * 3 + 3)
                for k in range(2):
                    for t in range(T):
                        dve.tensor_scalar(pick[:, k, t, :], iota_f[:], top_if[:, t, k:k + 1],
                                          w_top[:, k, t:t + 1], ALU.is_equal, ALU.mult).then_inc(s_pick, 1)
                dve.wait_ge(s_pick, u * 8 + 8)
                dve.tensor_tensor(cw[:], pick[:, 0, :, :], pick[:, 1, :, :], ALU.add).then_inc(s_cw, 1)
                dve.wait_ge(s_cw, u + 1)

            def experts(b, l):
                def add_expert(e):
                    n = EXPERTS[0] * l + e
                    dve.wait_ge(s_dn, b * N_DN + (n + 1))
                    if e:
                        dve.wait_ge(s_acc, b * (4 * N_DN) + (4 * n))
                    down = bank[e % 2][:].rearrange("p (t d) -> p t d", t=T)
                    for t in range(T):
                        if e == 0:
                            ins = dve.tensor_scalar(acc[:, t, :], down[:, t, :], cw[:, t, e:e + 1], None, ALU.mult)
                        elif e < E:
                            ins = dve.scalar_tensor_tensor(out=acc[:, t, :], in0=down[:, t, :],
                                                           scalar=cw[:, t, e:e + 1], in1=acc[:, t, :],
                                                           op0=ALU.mult, op1=ALU.add)
                        else:
                            ins = dve.tensor_tensor(acc[:, t, :], down[:, t, :], acc[:, t, :], ALU.add)
                        ins.then_inc(s_acc, 1)

                for i in range(UNITS[l]):
                    n = UNITS[0] * l + i
                    dve.wait_ge(s_sg, b * N_UNIT + (n + 1))
                    if i >= 3:
                        dve.wait_ge(s_dn, b * N_DN + (EXPERTS[0] * l + (i - 1) // 2))
                    dve.tensor_tensor(hid[:, i % 2, :], silu[:, i % 2, :], wide[i % 2][:, 1, :],
                                      ALU.mult).then_inc(s_hid, 1)
                    if i % HC == 1 and i > 1:
                        add_expert(i // HC - 1)
                add_expert(EXPERTS[l] - 1)
                u = b * 2 + l
                dve.wait_ge(s_acc, b * (4 * N_DN) + 4 * (EXPERTS[0] * l + EXPERTS[l]))
                gb = gate[:, l, bass.ds(b, 1), 1, :].to_broadcast([P, T, D])
                dve.tensor_tensor(gated[:], acc[:], gb, ALU.mult).then_inc(s_gy, 1)
                dve.wait_ge(s_gy, u + 1)
                dve.tensor_tensor(X[:], X[:], gated[:], ALU.add).then_inc(s_xe, 1)
                dve.wait_ge(s_xe, u + 1)

            dve.wait_ge(s_mod, 8)
            dve.wait_ge(s_gate, 5 * GATES)
            with dve.Fori(0, B) as b:
                dve.tensor_copy(modb[:].rearrange("p l w k -> p (l w k)"),
                                modT[:, :, :, :, bass.ds(b, 1)].rearrange("p l w k b -> p (l w k b)")
                                ).then_inc(s_modb, 1)
                dve.wait_ge(s_x, b * 16 + 16)
                norm(b, 0, 0)
                split_q(b, 0)
                for t in range(T):
                    for a in range(PAIRS):
                        n = t * PAIRS + a
                        lo, hi = P * NEAR[t][0], P * NEAR[t][1]
                        dve.wait_ge(s_S, b * N_S + (n + 1))
                        dve.reduce_max(M[:, t, a, :], wide[n % 2][:, :, lo:hi], AX.X).then_inc(s_mx, 1)
                dve.wait_ge(s_mx, b * N_S + N_MAX[0])
                split_max(b, 0)
                for g in range(GROUPS):
                    dve.wait_ge(s_pv, b * N_PV + T * (g + 1))
                    dve.tensor_copy(oT[:, g, :], bank[g % 2][:]).then_inc(s_oT, 1)
                finish_attention(b, 0)
                norm(b, 0, 1)
                route(b, 0)
                experts(b, 0)
                norm(b, 1, 0)
                split_q(b, 1)
                for t in range(T):
                    dve.wait_ge(s_S, b * N_S + (S1 + t + 1))
                    dve.reduce_max(M[:, t, :, :].rearrange("p a h -> p (a h)"),
                                   wide[t % 2][:].rearrange("p a (h s) -> p (a h) s", s=WIN),
                                   AX.X).then_inc(s_mx, 1)
                dve.wait_ge(s_mx, b * N_S + N_S)
                split_max(b, 1)
                dve.wait_ge(s_pv, b * N_PV + N_PV)
                for g in range(GROUPS):
                    dve.tensor_copy(oT[:, g, :], bank[g][:]).then_inc(s_oT, 1)
                finish_attention(b, 1)
                norm(b, 1, 1)
                route(b, 1)
                experts(b, 1)

        @block.tensor
        def _(pe):
            pe.wait_ge(s_w, N_SMALL)
            pe.wait_ge(s_cact, 1)
            for l in range(LAYERS):
                for w in range(2):
                    for k in range(2):
                        j = 3 * w + k
                        c0 = ((l * 2 + w) * 2 + k) * B
                        mm = pe.matmul(bank[0][:, c0:c0 + B], wmod_sb[:, l, j, :], c_act[:, l, :],
                                       start=True, stop=True)
            mm.then_inc(s_modps, 1)
            pe.wait_ge(s_crow, 2)
            for i in range(GATES):
                l, b = i // B, i % B
                if i >= 2:
                    pe.wait_ge(s_gate, 5 * (i - 2) + 3)
                for w in range(2):
                    mm = pe.matmul(bank[1 + i % 2][:, D * w:D * w + D], c_rows[:, l, b, :],
                                   wmod_sb[:, l, 3 * w + 2, :], start=True, stop=True)
                mm.then_inc(s_gps, 1)
            need = pe.to_reg(2)
            pe.wait_ge(s_const, N_CONST)
            pe.wait_ge(s_identb, need)
            pe.wait_ge(s_mod, 8)
            pe.wait_ge(s_gate, 5 * GATES)
            pe.wait_ge(s_ones, 64)
            pe.wait_ge(s_wb, 64)

            def transpose_norm(b, l, w):
                z = b * 4 + (2 * l + w)
                for t in range(T):
                    pe.wait_ge(s_xh, z * 4 + (t + 1))
                    mm = pe.transpose(bank[0][:, P * t:P * t + P], xh[:, t, :], ident[:])
                mm.then_inc(s_xT, 1)

            def project_qkv(b, l):
                u = b * 2 + l
                pe.wait_ge(s_hT, b * 4 + (2 * l + 1))
                pe.matmul(bank[1][:], wq_sb[l][:], hT[:], start=True, stop=True).then_inc(s_qps, 1)
                pe.matmul(bank[2][:], wk_sb[l][:], hT[:], start=True, stop=True).then_inc(s_kps, 1)
                for t in range(T):
                    mm = pe.matmul(bank[3][:, P * t:P * t + P], hT[:, P * t:P * t + P], wv_sb[l][:], start=True, stop=True)
                mm.then_inc(s_vps, 1)
                pe.wait_ge(s_qs, u * 128 + 128)
                pe.wait_ge(s_ks, u * 96 + 96)

            def transpose_max(b, l):
                u = b * 2 + l
                need = pe.to_reg(u * 4 + 4)
                pe.wait_ge(s_const, N_CONST)
                pe.wait_ge(s_msp, need)
                mT_ps = bank[0][:].bitcast(BF16)
                for t in range(T):
                    mm = pe.transpose(mT_ps[0:2 * PARTS * PAIRS, P * t:P * t + P],
                                      m_parts[:, t].rearrange("p h c a -> p (h c a)"), ident_b[:])
                mm.then_inc(s_mTp, 1)
                pe.wait_ge(s_mr, u * 32 + 32)
                pe.wait_ge(s_v, u + 1)

            def project_out(b, l):
                u = b * 2 + l
                pe.wait_ge(s_oT, u * 4 + 4)
                for t in range(T):
                    for g in range(GROUPS):
                        mm = pe.transpose(wide[t // 2][:, t % 2, P * g:P * g + P],
                                          oT[:, g, P * t:P * t + P], ident[:])
                    mm.then_inc(s_o, 1)
                for t in range(T):
                    pe.wait_ge(s_att, u * 4 + (t + 1))
                    mm = pe.transpose(bank[0][:, P * t:P * t + P], att[:, t, :], ident[:])
                mm.then_inc(s_aTp, 1)
                pe.wait_ge(s_aT, u + 1)
                for t in range(T):
                    mm = pe.matmul(bank[1][:, P * t:P * t + P], attT[:, P * t:P * t + P], wo_sb[l][:],
                                   start=True, stop=True)
                mm.then_inc(s_pr, 1)

            def experts(b, l):
                u = b * 2 + l
                pe.wait_ge(s_hT, b * 4 + (2 * l + 2))
                for t in range(T):
                    mm = pe.matmul(bank[2][:, E * t:E * t + E], hT[:, P * t:P * t + P], router_sb[l][:],
                                   start=True, stop=True)
                mm.then_inc(s_lg, 1)

                def down(i):
                    n = UNITS[0] * l + i
                    e, c = i // HC, i % HC
                    pe.wait_ge(s_hid, b * N_UNIT + (n + 1))
                    if c == 0 and e >= 2:
                        pe.wait_ge(s_acc, b * (4 * N_DN) + 4 * (EXPERTS[0] * l + e - 1))
                    for t in range(T):
                        mm = pe.matmul(bank[e % 2][:, P * t:P * t + P], hid[:, i % 2, P * t:P * t + P],
                                       wdn_sb[l][:, e, c, :], start=(c == 0 and t == 0), stop=True,
                                       skip_group_check=True)
                    if c == 1:
                        mm.then_inc(s_dn, 1)

                for i in range(UNITS[l]):
                    n = UNITS[0] * l + i
                    e, c = i // HC, i % HC
                    if i >= 2:
                        pe.wait_ge(s_hid, b * N_UNIT + (n - 1))
                    pe.matmul(wide[i % 2][:, 0, :], wup_sb[l][:, e, 0, P * c:P * c + P], hT[:],
                              start=True, stop=True)
                    pe.matmul(wide[i % 2][:, 1, :], wup_sb[l][:, e, 1, P * c:P * c + P], hT[:],
                              start=True, stop=True).then_inc(s_gu, 1)
                    if i:
                        down(i - 1)
                down(UNITS[l] - 1)

            with pe.Fori(0, B) as b:
                transpose_norm(b, 0, 0)
                project_qkv(b, 0)
                for t in range(T):
                    for a in range(PAIRS):
                        n = t * PAIRS + a
                        lo, hi = P * NEAR[t][0], P * NEAR[t][1]
                        k0 = P * CUT[t]
                        if n >= 2:
                            pe.wait_ge(s_mx, b * N_S + (n - 1))
                        for half in range(2):
                            pe.matmul(wide[n % 2][:, half, lo:hi], qs[:, a, P * t:P * t + P],
                                      ks[:, half, a, lo:hi], start=True, stop=True)
                        for half in range(2):
                            mm = pe.matmul(wide[n % 2][:, half, k0:k0 + P], ident_b[:],
                                           (cut_late if CUT[t] > t else cut_early)[:],
                                           start=False, stop=True, skip_group_check=True)
                        mm.then_inc(s_S, 1)
                transpose_max(b, 0)

                def scores(n):
                    g, kt = n // T, KEY_TILES[n % T]
                    lo, hi = P * NEAR[kt][0], P * NEAR[kt][1]
                    for two in range(2):
                        if n:
                            pe.wait_ge(s_ex, b * N_EX + (2 * n + two - 1))
                        for half in range(2):
                            a = 2 * g + two
                            mm = pe.matmul(wide[two][:, half, lo:hi], ks[:, half, a, P * kt:P * kt + P],
                                           qs[:, a, lo:hi], start=True, stop=True)
                        mm.then_inc(s_T, 1)

                def times_v(n):
                    g, i = n // T, n % T
                    kt = KEY_TILES[i]
                    lo, hi = P * NEAR[kt][0], P * NEAR[kt][1]
                    pe.wait_ge(s_cut, b * (GROUPS * T) + (n + 1))
                    if i == 0 and g >= 2:
                        pe.wait_ge(s_oT, b * 8 + (g - 1))
                    for j in range(4):
                        mm = pe.matmul(bank[g % 2][COL * j:COL * j + COL, lo:hi], V[:, kt, 4 * g + j, :],
                                       prob[:, n % 2, j, lo:hi], start=(i == 0), stop=True,
                                       skip_group_check=True)
                    mm.then_inc(s_pv, 1)

                for n in range(GROUPS * T):
                    scores(n)
                    if n:
                        times_v(n - 1)
                times_v(GROUPS * T - 1)
                project_out(b, 0)
                transpose_norm(b, 0, 1)
                experts(b, 0)

                transpose_norm(b, 1, 0)
                project_qkv(b, 1)
                for t in range(T):
                    if t >= 2:
                        pe.wait_ge(s_mx, b * N_S + (S1 + t - 1))
                    for h in range(HEADS):
                        a, half = h // 2, h % 2
                        for w in range(2):
                            r, c0 = WIN * w, P * t + WIN * w
                            mm = pe.matmul(wide[t % 2][r:r + WIN, h // 8, WIN * (h % 8):WIN * (h % 8) + WIN],
                                           qs[:, a, c0:c0 + WIN], ks[:, half, a, c0:c0 + WIN],
                                           start=True, stop=True)
                    mm.then_inc(s_S, 1)
                transpose_max(b, 1)

                def win_scores(t):
                    if t >= 2:
                        pe.wait_ge(s_ex, b * N_EX + (N_EXP[0] + 2 * (t - 1)))
                    for h in range(HEADS):
                        a, half = h // 2, h % 2
                        for w in range(2):
                            r, c0 = WIN * w, P * t + WIN * w
                            mm = pe.matmul(wide[t % 2][r:r + WIN, h // 8, WIN * (h % 8):WIN * (h % 8) + WIN],
                                           ks[:, half, a, c0:c0 + WIN], qs[:, a, c0:c0 + WIN],
                                           start=True, stop=True)
                    mm.then_inc(s_T, 1)

                def win_times_v(t):
                    pe.wait_ge(s_ex, b * N_EX + (N_EXP[0] + 2 * (t + 1)))
                    for g in range(GROUPS):
                        for j in range(4):
                            mm = pe.matmul(bank[g][COL * j:COL * j + COL, P * t:P * t + P],
                                           V[:, t, 4 * g + j, :], win_prob[:, t % 2, 4 * g + j, :],
                                           start=True, stop=True)
                    mm.then_inc(s_pv, 1)

                for t in range(T):
                    win_scores(t)
                    if t:
                        win_times_v(t - 1)
                win_times_v(T - 1)
                project_out(b, 1)
                transpose_norm(b, 1, 1)
                experts(b, 1)


def build(nc, arrays):
    aps = {n: nc.dram_tensor(n, a.shape, F32, kind="ExternalInput").ap() for n, a in arrays.items()}
    out = nc.dram_tensor("out", (B, SEQ, D), F32, kind="ExternalOutput").ap()
    two = {n: [aps[f"{n}{l}"] for l in range(LAYERS)]
           for n in ("cT", "wmod", "wq", "wk", "wv", "wo", "bq", "bk", "bv", "bo", "router", "wup", "wdn")}
    adaln_two_layers(nc, aps["x"], two["cT"], two["wmod"], two["wq"], two["wk"], two["wv"], two["wo"],
                     two["bq"], two["bk"], two["bv"], two["bo"], two["router"], aps["ebias"],
                     two["wup"], two["wdn"], out)


def layout(inputs):
    import numpy as np

    a = {n: np.asarray(v) for n, v in inputs.items()}

    def by_half(w):
        return w.reshape(-1, PAIRS, 2, HD).transpose(0, 2, 3, 1).reshape(-1, D)

    def up(*pairs):
        gu = [np.stack([g, u], 1) for g, u in pairs]
        w = np.concatenate(gu, 0)
        return w.transpose(2, 0, 1, 3).reshape(P, -1)

    def down(*ws):
        w = np.concatenate(ws, 0)
        return w.reshape(-1, HC, P, D).transpose(2, 0, 1, 3).reshape(P, -1)

    qkv, bqkv = a["L1_attn_w_qkv"], a["L1_attn_b_qkv"]
    got = {
        "x": a["L0_attn_hidden_states"],
        "cT0": a["L0_c"].T, "cT1": a["L1_c"].T, "wmod0": a["L0_wmod"], "wmod1": a["L1_wmod"],
        "wq0": by_half(a["L0_attn_wq"]), "wk0": by_half(a["L0_attn_wk"]),
        "wv0": a["L0_attn_wv"], "wo0": a["L0_attn_wo"],
        "bq0": by_half(a["L0_attn_bq"][None]).T, "bk0": by_half(a["L0_attn_bk"][None]).T,
        "bv0": a["L0_attn_bv"], "bo0": a["L0_attn_bo"],
        "wq1": by_half(qkv[:, 0:D]), "wk1": by_half(qkv[:, D:2 * D]), "wv1": qkv[:, 2 * D:],
        "wo1": a["L1_attn_w_out"],
        "bq1": by_half(bqkv[None, 0:D]).T, "bk1": by_half(bqkv[None, D:2 * D]).T, "bv1": bqkv[2 * D:],
        "bo1": a["L1_attn_b_out"],
        "router0": a["L0_ffn_router_w"].T, "router1": a["L1_ffn_gate_kernel"],
        "ebias": a["L0_ffn_experts_bias"],
        "wup0": up((a["L0_ffn_w1"], a["L0_ffn_w3"]), (a["L0_ffn_sw1"], a["L0_ffn_sw3"])),
        "wdn0": down(a["L0_ffn_w2"], a["L0_ffn_sw2"]),
        "wup1": up((a["L1_ffn_w0_kernel"], a["L1_ffn_w1_kernel"])),
        "wdn1": down(a["L1_ffn_wo_kernel"]),
    }
    return {n: np.ascontiguousarray(v) for n, v in got.items()}


def kernel(**inputs):
    import concourse.bacc as bacc
    from concourse.bass_utils import run_bass_kernel_spmd

    nc = bacc.Bacc("TRN2", target_bir_lowering=False, num_devices=1)
    arrays = layout(inputs)
    build(nc, arrays)
    r = run_bass_kernel_spmd(nc, [arrays], core_ids=[0])
    return r.results[0]["out"]
```

```python
from contextlib import ExitStack

import concourse.bass as bass
from concourse import mybir

F32 = mybir.dt.float32
F32R = mybir.dt.float32r
BF16 = mybir.dt.bfloat16
U32 = mybir.dt.uint32
ALU = mybir.AluOpType
ACT = mybir.ActivationFunctionType
AX = mybir.AxisListType

P = 128
B, SEQ, D = 4, 512, 128
LAYERS = 2
T = SEQ // P
HEADS, HD = 16, 8
PAIRS = HEADS // 2
E, HID = 8, 256
HC = HID // P
EXPERTS = [E + 1, E]
UNITS = [n * HC for n in EXPERTS]
UP, DOWN = 2 * HID, HC * D
WEXP = UP + DOWN
WIN, STRIDE = 64, 32
NWIN = SEQ // WIN
EPS = 1e-5
GATE_MIN = 0.25
SCALE = float(HD) ** -0.5
MASKED = -1e30

PARTS = 3
SLOTS = 6
TOP = SLOTS * HD
COL = 32
GROUPS = HEADS // 4
MROWS = 2 * PARTS * PAIRS

KEY_TILES = [1, 2, 0, 3]
NEAR = {0: (0, 3), 1: (0, 4), 2: (0, 4), 3: (1, 4)}
CUT = {0: 2, 1: 3, 2: 0, 3: 1}

N_EARLY = [8, 16]

LAG = 3

N_MAX = [T * PAIRS, T]
N_EXP = [GROUPS * T, T]


FIRST, LAYER_0, TURN, LAYER_1 = range(4)
WEIGHTS = [
    dict(max=1.75, norm=2, split_max=2, max_T=1.2, stack_max=2.5, norm_T=1.28, q=1.25, k=1,
         split=1.6, exp=1.5, pv=1.88, out_T=2.5, att_T=2, project=4, r_norm=1.5, r_norm_T=1.5,
         r_logits=3.75, r_route=1.5, r_route_T=1.5, r_route_out=1.5),
    dict(max=0.7, norm=2, split_max=2.5, max_T=2, stack_max=2, norm_T=0.29, q=0.6, k=3.12,
         split=0.48, exp=1.5, pv=1.88, out_T=2, att_T=2, project=2, r_norm=1.88, r_norm_T=0.6,
         r_logits=1.5, r_route=1.88, r_route_T=1.5, r_route_out=1.5),
    dict(max=1.92, norm=1.6, split_max=1.6, max_T=1.92, stack_max=2.5, norm_T=1.2, q=0.96, k=1.2,
         split=0.8, exp=2.5, pv=1.6, out_T=2, att_T=2.5, project=1.02, r_norm=5, r_norm_T=4,
         r_logits=4, r_route=0.16, r_route_T=1.28, r_route_out=1.54),
    dict(max=1.2, norm=6.25, split_max=5, max_T=3.84, stack_max=7.5, norm_T=2, q=0.9, k=2.56,
         split=5, exp=3.2, pv=5, out_T=4, att_T=3.84, project=0.6, r_norm=6.4, r_norm_T=3.2,
         r_logits=2.4, r_route=5, r_route_T=3.07, r_route_out=1.27),
]


def a(name, n=0, weight=2.0):
    return ("A", name, n, weight)


def nx(name, weight=2.0):
    return ("N", name, 0, weight)

def f(name, n=0, weight=3.0):
    return ("F", name, n, weight)


def w(n):
    return ("W", "w", n, 2.0)


def merged(main, side):
    out, done, k = [], 0.0, 0
    total, side_total = sum(s[3] for s in main), sum(s[3] for s in side)
    side_done = 0.0
    for step in main:
        out.append(step)
        done += step[3]
        while k < len(side) and side_done / side_total <= done / total:
            side_done += side[k][3]
            out.append(side[k])
            k += 1
    return out + side[k:]


def plan_start():
    return [nx(name) for name in ("norm", "norm_T", "q", "k", "split", "load", "bias", "v")]


def attention_steps(l, following, wt):
    def steps(make, *names):
        return [make(name, weight=wt[name]) for name in names]

    out = [a("max", n, wt["max"]) for n in range(N_MAX[l])]
    if following:
        out[-2:-2] = steps(nx, "norm")
    out += steps(a, "split_max", "max_T", "stack_max")
    out += steps(nx, "norm_T", "q", "k", "split") + [nx("bias", 0.0)] if following else []
    for n in range(N_EXP[l] + 1):
        out += [a("exp", n, wt["exp"])] if n < N_EXP[l] else []
        out += [a("pv", n - 1, wt["pv"])] if n else []
    out += [nx("load", 0.0)] if following else []
    out += steps(a, "out_T", "att_T")
    out += [nx("v", 0.0)] if following else []
    return out + steps(a, "project")


ROUTING = ("norm", "norm_T", "logits", "route", "route_T", "route_out")


def expert_steps(l):
    return ([f("split_h", 0, 1.0)] + [f("unit", i) for i in range(UNITS[l] + LAG)] + [f("out_T"), f("out")])


def plan_slot(la, lf, following, wt):
    main, side = attention_steps(la, following, wt), expert_steps(lf)
    if lf == 0:
        side = [f(name, 0, wt["r_" + name]) for name in ROUTING] + side
    if la == 1:
        main += [("R", name, 0, wt["r_" + name]) for name in ROUTING]
    if lf == 1:
        return side[:1] + merged(main, side[1:])
    return merged(main, side)


def plan_attention_and_weights():
    return merged(attention_steps(0, True, WEIGHTS[FIRST]), [w(n) for n in range(EXPERTS[0] + 1)])


def plan_turn():
    plan, n = [], 0
    for step in plan_slot(1, 0, True, WEIGHTS[TURN]):
        plan.append(step)
        if step[:2] == ("F", "unit") and step[2] >= 4 and step[2] % 2 == 0:
            plan.append(w(n))
            n += 1
    return plan + [w(i) for i in range(n, EXPERTS[1] + 1)]


def expert_of(l, i):
    k = i // HC
    return k if l == 1 else (E if k == 0 else k - 1)


def routed(l, i):
    return expert_of(l, i) < E


def upto(l, b, per_run, n):
    return l * B * per_run[0] + b * per_run[l] + n


def before(l, b, per_run):
    return upto(l, b, per_run, 0)


def adaln_two_layers(nc, x, cT, wmod, wq, wk, wv, wo, bq, bk, bv, bo, router, ebias, wexp, out):
    with ExitStack() as ctx:
        def sb(name, shape, dt=F32):
            return ctx.enter_context(nc.sbuf_tensor(name, shape, dt))

        def ps(name, shape, dt=F32):
            return ctx.enter_context(nc.psum_tensor(name, shape, dt))

        def sem(name):
            return ctx.enter_context(nc.semaphore(name))

        wq_sb = [sb(f"wq{l}_sb", [P, D]) for l in range(LAYERS)]
        wk_sb = [sb(f"wk{l}_sb", [P, D]) for l in range(LAYERS)]
        wv_sb = [sb(f"wv{l}_sb", [P, D]) for l in range(LAYERS)]
        wo_sb = [sb(f"wo{l}_sb", [P, D]) for l in range(LAYERS)]
        bq_sb = [sb(f"bq{l}_sb", [P, 1]) for l in range(LAYERS)]
        bk_sb = [sb(f"bk{l}_sb", [P, 1]) for l in range(LAYERS)]
        bv_sb = [sb(f"bv{l}_sb", [P, D]) for l in range(LAYERS)]
        bo_sb = [sb(f"bo{l}_sb", [P, D]) for l in range(LAYERS)]
        router_sb = [sb(f"router{l}_sb", [P, E]) for l in range(LAYERS)]
        ebias_sb = sb("ebias_sb", [P, E])
        w_raw = sb("w_raw", [P, 2, WEXP])
        w_hi = sb("w_hi", [P, E + 1, WEXP], F32R)
        w_lo = sb("w_lo", [P, E + 1, WEXP], F32R)
        cT_sb = sb("cT_sb", [P, LAYERS, B])
        c_act = sb("c_act", [P, LAYERS, B])
        modT = sb("modT", [P, LAYERS, 2, 2, B])
        gate = sb("gate", [P, LAYERS, B, 2, D])
        ident = sb("ident", [P, P])
        ident_b = sb("ident_b", [P, P], BF16)
        cut_late = sb("cut_late", [P, P], BF16)
        cut_early = sb("cut_early", [P, P], BF16)
        minus_half = sb("minus_half", [P, T])
        iota_i = sb("iota_i", [P, E], mybir.dt.int32)
        iota_f = sb("iota_f", [P, E])

        X = sb("X", [P, B, T, D])

        stats_a = sb("stats_a", [P, T, 6])
        mv_a = sb("mv_a", [P, T, 2])
        var_a = sb("var_a", [P, T])
        rstd_a = sb("rstd_a", [P, T])
        hT_a = sb("hT_a", [P, SEQ])
        gate_bo = sb("gate_bo", [P, D])
        qs = sb("qs", [P, PAIRS, SEQ], BF16)
        ks = sb("ks", [P, 2, PAIRS, SEQ], BF16)
        V = sb("V", [P, T, HEADS, COL])
        M = sb("M", [P, T, PAIRS, 2])
        m_rest = sb("m_rest", [P, T, PAIRS, 2])
        m_parts = sb("m_parts", [P, T, 2, PARTS, PAIRS], BF16)
        mT = sb("mT", [MROWS, SEQ], BF16)
        rden = sb("rden", [P, T, HEADS])
        early_a = sb("early_a", [P, 4, SEQ])
        qf, kf, q_rest, k_rest = (early_a[:, i, :] for i in range(4))
        oT = early_a
        parts_a = sb("parts_a", [P, 3, SEQ])
        parts_b = parts_a[:].rearrange("p c s -> p (c s)").bitcast(BF16).rearrange("p (c s) -> p c s", s=SEQ)
        q_parts, k_parts = parts_b[:, 0:PARTS, :], parts_b[:, PARTS:2 * PARTS, :]
        xh_a = parts_a[:, 0, :].rearrange("p (t d) -> p t d", t=T)
        att = parts_a[:, 0, :].rearrange("p (t d) -> p t d", t=T)
        attT = parts_a[:, 1, :]
        gated_a = parts_a[:, 2, :].rearrange("p (t d) -> p t d", t=T)
        probs = sb("probs", [P, 2, 4 * SEQ])
        prob = probs[:].rearrange("p c (h s) -> p c h s", s=SEQ)
        win_prob = probs[:].rearrange("p c (h s) -> p c h s", s=P)
        setup = probs[:].rearrange("p c n -> p (c n)")
        wmod_sb = setup[:, 0:LAYERS * 6 * D].rearrange("p (l j d) -> p l j d", l=LAYERS, j=6)
        gate_sign = setup[0:B, 12 * D:16 * D]
        gate_size = setup[0:B, 16 * D:20 * D]
        gate_rows = setup[0:B, 20 * D:24 * D]
        ones_b = early_a[0:PARTS, :, :].rearrange("p c s -> p (c s)").bitcast(BF16)

        stats_f = sb("stats_f", [P, T, 6])
        mv_f = sb("mv_f", [P, T, 2])
        var_f = sb("var_f", [P, T])
        rstd_f = sb("rstd_f", [P, T])
        xh_f = sb("xh_f", [P, T, D])
        hT_f = sb("hT_f", [P, SEQ])
        h_hi = sb("h_hi", [P, SEQ], F32R)
        h_lo = sb("h_lo", [P, SEQ], F32R)
        logit = sb("logit", [P, T, E])
        top = sb("top", [P, T, E])
        top_i = sb("top_i", [P, T, E], U32)
        top_if = sb("top_if", [P, T, 2])
        gap = sb("gap", [P, T])
        gap_e = sb("gap_e", [P, T])
        gap_s = sb("gap_s", [P, T])
        w_top = sb("w_top", [P, 2, T])
        pick = sb("pick", [P, 2, T, E])
        cw = sb("cw", [P, T, E])
        cwT = sb("cwT", [E, SEQ])
        cw_all = sb("cw_all", [P, E, SEQ])
        silu = sb("silu", [P, 2, SEQ])
        hid = sb("hid", [P, 2, SEQ])
        hid_w = sb("hid_w", [P, 2, SEQ])
        hid_hi = sb("hid_hi", [P, LAG + 1, SEQ], F32R)
        hid_lo = sb("hid_lo", [P, LAG + 1, SEQ], F32R)
        yT = silu[:, 0, :]
        gated_f = hid[:, 0, :].rearrange("p (t d) -> p t d", t=T)

        wide = [ps(f"wide{i}", [P, 2, SEQ]) for i in range(2)]
        side = ps("side", [P, SEQ])
        xT_ps = wide[1][:, 1, :]
        g_ps = ps("g_ps", [P, SEQ])
        u_ps = ps("u_ps", [P, SEQ])
        y_ps = ps("y_ps", [P, SEQ])

        q_dram = nc.dram_tensor("q_dram", (2, PARTS * HD + PARTS, PAIRS, SEQ), BF16, kind="Internal").ap()
        k_dram = nc.dram_tensor("k_dram", (2, PARTS * HD, PAIRS, SEQ), BF16, kind="Internal").ap()
        m_dram = nc.dram_tensor("m_dram", (2, PARTS, PAIRS, SEQ), BF16, kind="Internal").ap()
        gate_dram = nc.dram_tensor("gate_dram", (LAYERS, B, 2, D), F32, kind="Internal").ap()
        cw_dram = nc.dram_tensor("cw_dram", (E, SEQ), F32, kind="Internal").ap()

        s_c = sem("conditioning_loaded")
        s_w = sem("weights_loaded")
        s_const = sem("constants_made")
        s_zero = sem("buffers_zeroed")
        s_identb = sem("vector_constants_made")
        s_ones = sem("ones_placed")
        s_cact = sem("conditioning_activated")
        s_vset = sem("v_tile_set")
        s_modps = sem("modulation_in_psum")
        s_mod = sem("modulation_copied")
        s_gps = sem("gates_in_psum")
        s_gate = sem("gates_made")
        s_gw = sem("gates_stored")
        s_gl = sem("gates_spread")
        s_x0 = sem("first_x_loaded")
        s_x = sem("other_x_loaded")
        s_wd = [sem(f"raw_weights_{i}") for i in range(2)]
        s_whi = sem("weights_hi")
        s_wlo = sem("weights_lo")
        s_stat = sem("a_norm_stats")
        s_aggr = sem("a_norm_mean_var")
        s_var = sem("a_norm_var_eps")
        s_rstd = sem("a_norm_rstd")
        s_xh = sem("a_normalised")
        s_xT = sem("a_normalised_T_psum")
        s_hT = sem("a_hT_ready")
        s_qps = sem("q_psum")
        s_kps = sem("k_psum")
        s_vps = sem("v_psum")
        s_qf = sem("q_copied")
        s_kf = sem("k_copied")
        s_qsp = sem("q_split")
        s_ksp = sem("k_split")
        s_v = sem("v_copied")
        s_qw = sem("q_parts_stored")
        s_kw = sem("k_parts_stored")
        s_qs = sem("q_stack_loaded")
        s_ks = sem("k_stack_loaded")
        s_S = sem("scores_for_max")
        s_mx = sem("max_taken")
        s_msp = sem("max_split")
        s_mTp = sem("max_T_psum")
        s_mT = sem("max_T_copied")
        s_mw = sem("max_stored")
        s_mr = sem("max_stacked")
        s_T = sem("scores_for_exp")
        s_ex = sem("exp_done")
        s_cut = sem("band_cut")
        s_pv = sem("pv_done")
        s_oT = sem("oT_copied")
        s_o = sem("o_psum")
        s_rden = sem("denominator_inverse")
        s_att = sem("attention_normed")
        s_aTp = sem("attention_T_psum")
        s_aT = sem("attention_T_copied")
        s_pr = sem("projected")
        s_gb = sem("gated_bias")
        s_gbo = sem("bias_added")
        s_gx = sem("gated_attention")
        s_xa = sem("x_after_attention")
        s_winz = sem("window_probs_zeroed")
        f_stat = sem("f_norm_stats")
        f_aggr = sem("f_norm_mean_var")
        f_var = sem("f_norm_var_eps")
        f_rstd = sem("f_norm_rstd")
        f_xh = sem("f_normalised")
        f_xT = sem("f_normalised_T_psum")
        f_hT = sem("f_hT_ready")
        f_hhi = sem("h_hi_ready")
        f_hlo = sem("h_lo_ready")
        f_lg = sem("logits_psum")
        f_lb = sem("logits_ready")
        f_m8 = sem("top_values")
        f_ix = sem("top_indices")
        f_gap = sem("top_gap")
        f_if = sem("top_indices_float")
        f_ge = sem("top_gap_exp")
        f_w12 = sem("top_weights")
        f_pick = sem("picked")
        f_cw = sem("token_weights")
        f_cwp = sem("token_weights_T_psum")
        f_cwT = sem("token_weights_T")
        f_cwd = sem("token_weights_stored")
        f_cwa = [sem(f"token_weights_spread_{e}") for e in range(E)]
        f_g = sem("gate_psum")
        f_u = sem("up_psum")
        f_th = sem("gate_tanh")
        f_sg = sem("silu_done")
        f_hid = sem("hidden_ready")
        f_hw = sem("hidden_weighted")
        f_hi = sem("hidden_hi_by_act")
        f_lo = sem("hidden_lo_by_pool")
        f_hiv = sem("hidden_hi_by_vector")
        f_lov = sem("hidden_lo_by_vector")
        f_dn = sem("down_done")
        f_yT = sem("yT_copied")
        f_y = sem("y_psum")
        f_gy = sem("gated_experts")
        f_xe = sem("x_after_experts")
        s_out = sem("stored")

        ONE, THREE, FOUR, EIGHT = [1, 1], [3, 3], [4, 4], [8, 8]
        DMA1, DMA2, DMA_Q, DMA_K = [16, 16], [32, 32], [128, 128], [96, 96]
        N_T = [2 * N_EXP[0], N_EXP[1]]
        N_EX = [2 * N_EXP[0], 2 * N_EXP[1]]
        N_ROUTED = [E * HC, E * HC]
        N_LATE = [UNITS[l] - N_EARLY[l] for l in range(LAYERS)]
        N_CONST = 9
        N_C = 16 * 2 * LAYERS
        N_W = 16 * (9 * LAYERS + 1)

        def wait_apart(eng, sem_, value):
            if isinstance(value, int):
                eng.wait_ge(sem_, value)
                return
            need = eng.to_reg(value)
            eng.wait_ge(s_const, N_CONST)
            eng.wait_ge(sem_, need)

        def early(l, b, i):
            return i < N_EARLY[l] and not last(l, b)

        def late_count(l, b, i):
            return upto(l, b, N_LATE, i + 1 - (0 if last(l, b) else N_EARLY[l]))

        def wait_split(eng, l, b, i):
            if early(l, b, i):
                eng.wait_ge(f_lo, upto(l, b, N_EARLY, i + 1))
            else:
                eng.wait_ge(f_lov, late_count(l, b, i))

        def before_hi(eng, l, b, i):
            if i > LAG:
                eng.wait_ge(f_dn, upto(l, b, UNITS, i - LAG))
            if routed(l, i):
                eng.wait_ge(f_hw, upto(l, b, N_ROUTED, i + 1 - (HC if l == 0 else 0)))
                return hid_w[:, i % 2, :]
            eng.wait_ge(f_hid, upto(l, b, UNITS, i + 1))
            return hid[:, i % 2, :]

        def g_tile(l, b, n):
            return wide[0][:, 0, :] if last(l, b) and n % 2 else g_ps[:]

        def windows(tile):
            first = tile[:, 0:WIN]
            return bass.AP(first.tensor, first.offset, [list(first.ap[0]), [STRIDE, NWIN], [1, WIN]])

        def lot(ap, b):
            return ap[:, b] if isinstance(b, int) else ap[:, bass.ds(b, 1)]

        def x_of(b):
            return X[:, b] if isinstance(b, int) else X[:, bass.ds(b, 1)].rearrange("p o t d -> p (o t) d")

        def gate_of(l, b, w):
            g = gate[:, l, b:b + 1, w, :] if isinstance(b, int) else gate[:, l, bass.ds(b, 1), w, :]
            return g

        def mod_of(l, b, w, k):
            return modT[:, l, w, k, b:b + 1] if isinstance(b, int) else modT[:, l, w, k, bass.ds(b, 1)]

        def first(l, b):
            return l == 0 and isinstance(b, int) and b == 0

        def last(l, b):
            return l == LAYERS - 1 and isinstance(b, int) and b == B - 1

        def run(eng, step_of):
            def slot(plan, att=None, ffn=None, nxt=None, second=False):
                at = {"A": att, "R": att, "F": ffn, "N": nxt, "W": (second,)}
                for stream, name, n, _ in plan:
                    step_of[stream](name, n, *at[stream])

            slot(plan_start(), nxt=(0, 0))
            slot(plan_attention_and_weights(), att=(0, 0), nxt=(0, 1))
            with eng.Fori(0, B - 2) as i:
                slot(plan_slot(0, 0, True, WEIGHTS[LAYER_0]), att=(0, i + 1), ffn=(0, i), nxt=(0, i + 2))
            slot(plan_slot(0, 0, True, WEIGHTS[LAYER_0]), att=(0, B - 1), ffn=(0, B - 2), nxt=(1, 0))
            slot(plan_turn(), att=(1, 0), ffn=(0, B - 1), nxt=(1, 1), second=True)
            with eng.Fori(0, B - 2) as i:
                slot(plan_slot(1, 1, True, WEIGHTS[LAYER_1]), att=(1, i + 1), ffn=(1, i), nxt=(1, i + 2))
            slot(plan_slot(1, 1, False, WEIGHTS[LAYER_1]), att=(1, B - 1), ffn=(1, B - 2))
            slot(expert_steps(1), ffn=(1, B - 1))

        block = ctx.enter_context(nc.Block())

        @block.sync
        def _(sp):
            for l in range(LAYERS):
                sp.dma_start(cT_sb[:, l, :], cT[l]).then_inc(s_c, 16)
                sp.dma_start(wmod_sb[:, l, :, :].rearrange("p j f -> p (j f)"), wmod[l]).then_inc(s_c, 16)
            xs = x.rearrange("b (t p) d -> p b t d", p=P)
            sp.dma_start(X[:, 0], xs[:, 0]).then_inc(s_x0, 16)
            for l in range(LAYERS):
                for dst, src in ((wq_sb, wq), (wk_sb, wk), (wv_sb, wv), (wo_sb, wo), (bq_sb, bq),
                                 (bk_sb, bk), (router_sb, router)):
                    sp.dma_start(dst[l][:], src[l]).then_inc(s_w, 16)
                for dst, src in ((bv_sb, bv), (bo_sb, bo)):
                    sp.dma_start(dst[l][:], src[l].partition_broadcast(P)).then_inc(s_w, 16)
            sp.dma_start(ebias_sb[:], ebias.partition_broadcast(P)).then_inc(s_w, 16)
            sp.wait_ge(s_const, 1)
            sp.wait_ge(s_zero, 1)
            for half in range(2):
                r = 64 * half + TOP
                sp.dma_start(ks[r:r + PARTS, half, :, :].rearrange("p a s -> p (a s)"),
                             ones_b).then_inc(s_ones, 16)
                sp.dma_start(q_dram[half, PARTS * HD:, :, :].rearrange("p a s -> p (a s)"),
                             qs[0:PARTS, :, :].rearrange("p a s -> p (a s)")).then_inc(s_ones, 16)
            sp.wait_ge(s_gate, 4)
            sp.dma_start(gate_dram.rearrange("l b w d -> b l w d"),
                         gate_rows.rearrange("b (l w d) -> b l w d", l=LAYERS, w=2)).then_inc(s_gw, 16)
            sp.wait_ge(s_gw, 16)
            sp.dma_start(gate[:].rearrange("p l b w d -> p (l b w d)"),
                         gate_dram.rearrange("l b w d -> (l b w d)").partition_broadcast(P)).then_inc(s_gl, 16)
            for b in range(1, B):
                sp.dma_start(X[:, b], xs[:, b]).then_inc(s_x, 16)

            def start(name, n, l, b):
                if name == "split":
                    sp.wait_ge(s_qsp, upto(l, b, FOUR, 4))
                    for half in range(2):
                        sp.dma_start(q_dram[half, 0:PARTS * HD, :, :].rearrange("(c d) a s -> (d a) c s", d=HD),
                                     q_parts[64 * half:64 * half + 64, :, :]).then_inc(s_qw, 16)
                    sp.wait_ge(s_ksp, upto(l, b, FOUR, 4))
                    for half in range(2):
                        sp.dma_start(k_dram[half].rearrange("(c d) a s -> (d a) c s", d=HD),
                                     k_parts[64 * half:64 * half + 64, :, :]).then_inc(s_kw, 16)
                elif name == "load":
                    q_stored = sp.to_reg(upto(l, b, DMA2, 32))
                    if not first(l, b):
                        wait_apart(sp, s_T, before(l, b, N_T))
                    sp.wait_ge(s_qw, q_stored)
                    for half in range(2):
                        r = 64 * half
                        q_h = q_dram[half].rearrange("r a s -> r (a s)")
                        qs_h = qs[:, :, :].rearrange("p a s -> p (a s)")
                        sp.dma_start(qs_h[r:r + 24, :], q_h[0:24, :]).then_inc(s_qs, 16)
                        sp.dma_start(qs_h[r + 24:r + 32, :], q_h[0:8, :]).then_inc(s_qs, 16)
                        sp.dma_start(qs_h[r + 32:r + 40, :], q_h[16:24, :]).then_inc(s_qs, 16)
                        sp.dma_start(qs_h[r + 40:r + 51, :], q_h[16:27, :]).then_inc(s_qs, 16)
                    sp.wait_ge(s_kw, upto(l, b, DMA2, 32))
                    for half in range(2):
                        r = 64 * half
                        k_h = k_dram[half].rearrange("r a s -> r (a s)")
                        ks_h = ks[:, half, :, :].rearrange("p a s -> p (a s)")
                        sp.dma_start(ks_h[r:r + 16, :], k_h[0:16, :]).then_inc(s_ks, 16)
                        sp.dma_start(ks_h[r + 16:r + 32, :], k_h[0:16, :]).then_inc(s_ks, 16)
                        sp.dma_start(ks_h[r + 32:r + 48, :], k_h[8:24, :]).then_inc(s_ks, 16)

            def attention(name, n, l, b):
                if name == "stack_max":
                    sp.wait_ge(s_mT, upto(l, b, ONE, 1))
                    sp.dma_start(m_dram.rearrange("h c a s -> (h c a) s"), mT[:]).then_inc(s_mw, 16)
                    sp.wait_ge(s_mw, upto(l, b, DMA1, 16))
                    for half in range(2):
                        r = 64 * half + TOP
                        sp.dma_start(qs[r:r + PARTS, :, :].rearrange("p a s -> p (a s)"),
                                     m_dram[half].rearrange("c a s -> c (a s)")).then_inc(s_mr, 16)

            def experts(name, n, l, b):
                if name == "route_T":
                    sp.wait_ge(f_cwT, upto(l, b, ONE, 1))
                    sp.dma_start(cw_dram, cwT[:]).then_inc(f_cwd, 16)
                elif name == "route_out":
                    wait_apart(sp, f_cwd, upto(l, b, DMA1, 16))
                    for e in range(E):
                        if l == 1:
                            wait_apart(sp, f_hw, before(l, b, N_ROUTED) - HC * (E - 1 - e))
                        sp.dma_start(cw_all[:, e, :], cw_dram[e].partition_broadcast(P)).then_inc(f_cwa[e], 16)
                elif name == "out" and l == 1:
                    sp.wait_ge(f_xe, upto(l, b, ONE, 1))
                    dst = out[b:b + 1] if isinstance(b, int) else out[bass.ds(b, 1)]
                    src = X[:, b:b + 1] if isinstance(b, int) else X[:, bass.ds(b, 1)]
                    sp.dma_start(dst.rearrange("b (t p) d -> p b t d", p=P), src).then_inc(s_out, 16)

            def weights(name, n, second):
                if n < EXPERTS[second]:
                    k = EXPERTS[0] * second + n
                    if k >= 2:
                        sp.wait_ge(s_wlo, k - 1)
                    src = wexp[second][:, expert_of(second, HC * n) * WEXP:(expert_of(second, HC * n) + 1) * WEXP]
                    sp.dma_start(w_raw[:, k % 2, :], src).then_inc(s_wd[k % 2], 16)

            run(sp, {"A": attention, "N": start, "R": experts, "F": experts, "W": weights})
            sp.wait_ge(s_out, 16 * B)

        @block.gpsimd
        def _(pool):
            pool.memset(ones_b, 1.0).then_inc(s_const, 1)
            pool.memset(ident[:], 0.0).then_inc(s_const, 1)
            pool.memset(cut_late[:], 0.0).then_inc(s_const, 1)
            pool.memset(cut_early[:], 0.0).then_inc(s_const, 1)
            pool.memset(minus_half[:], -0.5).then_inc(s_const, 1)
            pool.wait_ge(s_const, 5)
            pool.affine_select(out=ident[:], in_=ident[:], compare_op=ALU.not_equal, fill=1.0, base=0,
                               pattern=[[-1, P]], channel_multiplier=1).then_inc(s_const, 1)
            pool.affine_select(out=cut_late[:], in_=cut_late[:], compare_op=ALU.is_ge, fill=MASKED, base=0,
                               pattern=[[-1, P]], channel_multiplier=1).then_inc(s_const, 1)
            pool.affine_select(out=cut_early[:], in_=cut_early[:], compare_op=ALU.is_ge, fill=MASKED, base=0,
                               pattern=[[1, P]], channel_multiplier=-1).then_inc(s_const, 1)
            pool.iota(iota_i[:], pattern=[[1, E]], base=0, channel_multiplier=0).then_inc(s_const, 1)

            def start(name, n, l, b):
                if name == "norm":
                    wait_apart(pool, s_aggr, upto(l, b, FOUR, 4))
                    pool.tensor_scalar(var_a[:], mv_a[:, :, 1], EPS, None, ALU.add).then_inc(s_var, 1)
                    pool.wait_ge(s_var, upto(l, b, ONE, 1))
                    pool.tensor_tensor(rstd_a[:], var_a[:], minus_half[:], ALU.pow).then_inc(s_rstd, 1)
                elif name == "bias":
                    if first(l, b):
                        pool.wait_ge(s_w, N_W)
                        pool.wait_ge(s_gl, 16)
                    pool.tensor_tensor(gate_bo[:], gate_of(l, b, 0), bo_sb[l][:], ALU.mult).then_inc(s_gb, 1)
                    wait_apart(pool, s_gb, upto(l, b, ONE, 1))
                    wait_apart(pool, s_xh, upto(l, b, FOUR, 4))
                    pool.tensor_tensor(x_of(b), x_of(b), gate_bo[:].unsqueeze(1).to_broadcast([P, T, D]),
                                       ALU.add).then_inc(s_gbo, 1)

            def attention(name, n, l, b):
                if name == "exp" and l == 0:
                    kt = KEY_TILES[n % T]
                    wait_apart(pool, s_ex, upto(l, b, N_EX, 2 * n + 2))
                    cut = prob[:, n % 2, :, P * CUT[kt]:P * CUT[kt] + P]
                    sign = 1 if CUT[kt] > kt else -1
                    pool.affine_select(out=cut, in_=cut, compare_op=ALU.is_ge, fill=0.0, base=0,
                                       pattern=[[0, 4], [-sign, P]], channel_multiplier=sign).then_inc(s_cut, 1)

            def experts(name, n, l, b):
                if name == "norm":
                    wait_apart(pool, f_aggr, upto(l, b, FOUR, 4))
                    pool.tensor_scalar(var_f[:], mv_f[:, :, 1], EPS, None, ALU.add).then_inc(f_var, 1)
                    pool.wait_ge(f_var, upto(l, b, ONE, 1))
                    pool.tensor_tensor(rstd_f[:], var_f[:], minus_half[:], ALU.pow).then_inc(f_rstd, 1)
                elif name == "split_h":
                    pool.wait_ge(f_hhi, upto(l, b, ONE, 1))
                    pool.tensor_tensor(h_lo[:], hT_f[:], h_hi[:].bitcast(F32), ALU.subtract).then_inc(f_hlo, 1)
                elif name == "unit":
                    if n < UNITS[l] and routed(l, n):
                        if n % HC == 0:
                            pool.wait_ge(f_cwa[expert_of(l, n)], upto(l, b, DMA1, 16))
                        if n >= 2:
                            wait_split(pool, l, b, n - 2)
                        pool.wait_ge(f_hid, upto(l, b, UNITS, n + 1))
                        pool.tensor_tensor(hid_w[:, n % 2, :], hid[:, n % 2, :], cw_all[:, expert_of(l, n), :],
                                           ALU.mult).then_inc(f_hw, 1)
                    i = n - 1
                    if 0 <= i < UNITS[l] and early(l, b, i):
                        pool.wait_ge(f_hi, upto(l, b, N_EARLY, i + 1))
                        src = hid_w if routed(l, i) else hid
                        pool.tensor_tensor(hid_lo[:, i % (LAG + 1), :], src[:, i % 2, :], hid_hi[:, i % (LAG + 1), :].bitcast(F32),
                                           ALU.subtract).then_inc(f_lo, 1)

            def weights(name, n, second):
                if n >= 1:
                    k = EXPERTS[0] * second + n - 1
                    e = expert_of(second, HC * (n - 1))
                    pool.wait_ge(s_whi, k + 1)
                    pool.tensor_tensor(w_lo[:, e, :], w_raw[:, k % 2, :], w_hi[:, e, :].bitcast(F32),
                                       ALU.subtract).then_inc(s_wlo, 1)

            run(pool, {"A": attention, "N": start, "R": experts, "F": experts, "W": weights})

        @block.scalar
        def _(act):
            act.wait_ge(s_c, N_C)
            act.activation(c_act[:], cT_sb[:], ACT.Silu).then_inc(s_cact, 1)
            act.wait_ge(s_mod, 2 * 2 * LAYERS)
            act.wait_ge(s_w, N_W)

            def start(name, n, l, b):
                if name == "norm_T":
                    wait_apart(act, s_xT, upto(l, b, ONE, 1))
                    dst = hT_a[:].rearrange("p (n s) -> p n s", s=WIN) if l == 1 else hT_a[:]
                    act.activation(dst, windows(xT_ps) if l == 1 else xT_ps, ACT.Identity,
                                   bias=mod_of(l, b, 0, 0), scale=mod_of(l, b, 0, 1)).then_inc(s_hT, 1)
                elif name == "q":
                    if first(l, b):
                        act.wait_ge(s_ones, 64)
                    act.wait_ge(s_qps, upto(l, b, ONE, 1))
                    act.activation(qf, wide[0][:, 0, :], ACT.Identity, bias=bq_sb[l][:]).then_inc(s_qf, 1)
                elif name == "k":
                    act.wait_ge(s_kps, upto(l, b, ONE, 1))
                    act.activation(kf, wide[0][:, 1, :], ACT.Identity, bias=bk_sb[l][:]).then_inc(s_kf, 1)

            def attention(name, n, l, b):
                if name == "exp" and l == 0:
                    lo, hi = (P * k for k in NEAR[KEY_TILES[n % T]])
                    for two in range(2):
                        act.wait_ge(s_T, upto(l, b, N_T, 2 * n + two + 1))
                        if n >= 2:
                            act.wait_ge(s_pv, upto(l, b, N_EXP, n - 1))
                        act.activation(prob[:, n % 2, 2 * two:2 * two + 2, lo:hi], wide[two][:, :, lo:hi],
                                       ACT.Exp, scale=SCALE).then_inc(s_ex, 1)
                elif name == "exp" and l == 1:
                    act.wait_ge(s_T, upto(l, b, N_T, n + 1))
                    if n == 0:
                        act.wait_ge(s_winz, 1)
                    if n >= 2:
                        act.wait_ge(s_pv, upto(l, b, N_EXP, n - 1))
                    for w_ in range(2):
                        r = WIN * w_
                        act.activation(win_prob[r:r + WIN, n % 2, :, r:r + WIN],
                                       wide[n % 2][r:r + WIN, :, :].rearrange("p a (h s) -> p (a h) s", s=WIN),
                                       ACT.Exp, scale=SCALE).then_inc(s_ex, 1)
                elif name == "att_T":
                    act.wait_ge(s_aTp, upto(l, b, ONE, 1))
                    act.activation(attT, side[:], ACT.Identity).then_inc(s_aT, 1)

            def experts(name, n, l, b):
                if name == "norm_T":
                    wait_apart(act, f_xT, upto(l, b, ONE, 1))
                    act.activation(hT_f[:], side[:], ACT.Identity, bias=mod_of(l, b, 1, 0),
                                   scale=mod_of(l, b, 1, 1)).then_inc(f_hT, 1)
                elif name == "logits":
                    act.wait_ge(f_gap, upto(l, b, ONE, 1))
                    act.activation(gap_e[:], gap[:], ACT.Exp).then_inc(f_ge, 1)
                elif name == "unit":
                    if n < UNITS[l]:
                        act.wait_ge(f_g, upto(l, b, UNITS, n + 1))
                        if n >= 2:
                            act.wait_ge(f_hid, upto(l, b, UNITS, n - 1))
                        act.activation(silu[:, n % 2, :], g_tile(l, b, n), ACT.Tanh, scale=0.5).then_inc(f_th, 1)
                    i = n - 1
                    if 0 <= i < UNITS[l] and (early(l, b, i) or last(l, b)):
                        src = before_hi(act, l, b, i)
                        act.activation(hid_hi[:, i % (LAG + 1), :], src, ACT.Copy).then_inc(f_hi, 1)
                elif name == "out_T":
                    act.wait_ge(f_dn, upto(l, b, UNITS, UNITS[l]))
                    act.activation(yT, y_ps[:], ACT.Identity).then_inc(f_yT, 1)

            def weights(name, n, second):
                if n >= 1:
                    k = EXPERTS[0] * second + n - 1
                    e = expert_of(second, HC * (n - 1))
                    if second:
                        act.wait_ge(f_dn, (B - 1) * UNITS[0] + HC * (e + 2))
                    act.wait_ge(s_wd[k % 2], 16 * (k // 2 + 1))
                    act.activation(w_hi[:, e, :], w_raw[:, k % 2, :], ACT.Copy).then_inc(s_whi, 1)

            run(act, {"A": attention, "N": start, "R": experts, "F": experts, "W": weights})

        @block.vector
        def _(dve):
            dve.memset(qs[:].rearrange("p a s -> p (a s)").bitcast(U32), 0)
            dve.memset(ks[:].rearrange("p c a s -> p (c a s)").bitcast(U32), 0).then_inc(s_zero, 1)
            dve.wait_ge(s_modps, 1)
            mod_ps = wide[0][:, 0, 0:LAYERS * 4 * B].rearrange("p (l w k b) -> p l w k b", l=LAYERS, w=2, k=2)
            for l in range(LAYERS):
                for w_ in range(2):
                    dve.tensor_copy(modT[:, l, w_, 0, :], mod_ps[:, l, w_, 0, :]).then_inc(s_mod, 1)
                    dve.tensor_scalar(modT[:, l, w_, 1, :], mod_ps[:, l, w_, 1, :], 1.0, None,
                                      ALU.add).then_inc(s_mod, 1)
            dve.wait_ge(s_gps, 1)
            gate_raw = wide[1][0:B, 0, :]
            dve.tensor_scalar(gate_sign, gate_raw, 0.0, 0.5, ALU.is_ge, ALU.subtract).then_inc(s_gate, 1)
            dve.tensor_scalar(gate_size, gate_raw, -1.0, GATE_MIN, ALU.mult, ALU.max).then_inc(s_gate, 1)
            dve.wait_ge(s_gate, 2)
            dve.tensor_tensor(gate_size, gate_raw, gate_size, ALU.max).then_inc(s_gate, 1)
            dve.wait_ge(s_gate, 3)
            dve.scalar_tensor_tensor(out=gate_rows, in0=gate_size, scalar=2.0, in1=gate_sign,
                                     op0=ALU.mult, op1=ALU.mult).then_inc(s_gate, 1)
            dve.wait_ge(s_const, N_CONST)
            dve.tensor_copy(iota_f[:], iota_i[:])
            dve.tensor_copy(ident_b[:], ident[:]).then_inc(s_identb, 1)

            def normalise(l, b, stats, mv, rstd, xh, t_stat, t_aggr):
                for t in range(T):
                    wait_apart(dve, t_stat, upto(l, b, FOUR, t + 1))
                    dve.bn_aggr(mv[:, t, :], stats[:, t, :]).then_inc(t_aggr, 1)

            def x_tile(b, t):
                return X[:, b, t, :] if isinstance(b, int) else X[:, bass.ds(b, 1), t, :].rearrange("p o d -> p (o d)")

            def start(name, n, l, b):
                if name == "norm":
                    if l == 1:
                        wait_apart(dve, f_xe, b + 1)
                    elif first(l, b):
                        dve.wait_ge(s_x0, 16)
                    else:
                        dve.wait_ge(s_x, 16 * (B - 1))
                    for t in range(T):
                        dve.bn_stats(stats_a[:, t, :], x_tile(b, t)).then_inc(s_stat, 1)
                    normalise(l, b, stats_a, mv_a, rstd_a, xh_a, s_stat, s_aggr)
                elif name == "norm_T":
                    wait_apart(dve, s_rstd, upto(l, b, ONE, 1))
                    for t in range(T):
                        dve.tensor_scalar(xh_a[:, t, :], x_tile(b, t), mv_a[:, t, 0:1], rstd_a[:, t:t + 1],
                                          ALU.subtract, ALU.mult).then_inc(s_xh, 1)
                elif name == "split":
                    dve.wait_ge(s_qf, upto(l, b, ONE, 1))
                    dve.tensor_copy(q_parts[:, 2, :], qf).then_inc(s_qsp, 1)
                    dve.wait_ge(s_kf, upto(l, b, ONE, 1))
                    dve.tensor_copy(k_parts[:, 0, :], kf).then_inc(s_ksp, 1)
                    dve.wait_ge(s_qsp, upto(l, b, FOUR, 1))
                    dve.tensor_tensor(q_rest, qf, q_parts[:, 2, :], ALU.subtract).then_inc(s_qsp, 1)
                    dve.wait_ge(s_ksp, upto(l, b, FOUR, 1))
                    dve.tensor_tensor(k_rest, kf, k_parts[:, 0, :], ALU.subtract).then_inc(s_ksp, 1)
                    dve.wait_ge(s_qsp, upto(l, b, FOUR, 2))
                    dve.tensor_copy(q_parts[:, 0, :], q_rest).then_inc(s_qsp, 1)
                    dve.wait_ge(s_ksp, upto(l, b, FOUR, 2))
                    dve.tensor_copy(k_parts[:, 1, :], k_rest).then_inc(s_ksp, 1)
                    dve.wait_ge(s_qsp, upto(l, b, FOUR, 3))
                    dve.tensor_tensor(q_parts[:, 1, :], q_rest, q_parts[:, 0, :], ALU.subtract).then_inc(s_qsp, 1)
                    dve.wait_ge(s_ksp, upto(l, b, FOUR, 3))
                    dve.tensor_tensor(k_parts[:, 2, :], k_rest, k_parts[:, 1, :], ALU.subtract).then_inc(s_ksp, 1)
                elif name == "v":
                    dve.wait_ge(s_vps, upto(l, b, ONE, 1))
                    if first(l, b):
                        dve.memset(V[:], 0.0).then_inc(s_vset, 1)
                        dve.wait_ge(s_vset, 1)
                        dve.memset(V[:, :, :, HD:HD + 1], 1.0).then_inc(s_vset, 1)
                        dve.wait_ge(s_vset, 2)
                    for t in range(T):
                        v = dve.tensor_tensor(V[:, t, :, 0:HD],
                                              wide[1][:, 0, P * t:P * t + P].rearrange("p (h d) -> p h d", d=HD),
                                              bv_sb[l][:].rearrange("p (h d) -> p h d", d=HD), ALU.add)
                    v.then_inc(s_v, 1)

            def attention(name, n, l, b):
                if name == "max":
                    dve.wait_ge(s_S, upto(l, b, N_MAX, n + 1))
                    if l == 0:
                        t, pair = n // PAIRS, n % PAIRS
                        lo, hi = (P * k for k in NEAR[t])
                        dve.reduce_max(M[:, t, pair, :], wide[n % 2][:, :, lo:hi], AX.X).then_inc(s_mx, 1)
                    else:
                        dve.reduce_max(M[:, n, :, :].rearrange("p a h -> p (a h)"),
                                       wide[n % 2][:].rearrange("p a (h s) -> p (a h) s", s=WIN),
                                       AX.X).then_inc(s_mx, 1)
                elif name == "split_max":
                    dve.wait_ge(s_mx, upto(l, b, N_MAX, N_MAX[l]))
                    m = M[:].rearrange("p t a h -> p t h a")
                    rest = m_rest[:].rearrange("p t a h -> p t h a")
                    dve.tensor_scalar(m_parts[:, :, :, 0, :], m, -1.0, None, ALU.mult)
                    dve.tensor_scalar(rest, m, -1.0, None, ALU.mult).then_inc(s_msp, 1)
                    dve.wait_ge(s_msp, upto(l, b, FOUR, 1))
                    dve.tensor_tensor(rest, rest, m_parts[:, :, :, 0, :], ALU.subtract).then_inc(s_msp, 1)
                    dve.wait_ge(s_msp, upto(l, b, FOUR, 2))
                    dve.tensor_copy(m_parts[:, :, :, 1, :], rest).then_inc(s_msp, 1)
                    dve.wait_ge(s_msp, upto(l, b, FOUR, 3))
                    dve.tensor_tensor(m_parts[:, :, :, 2, :], rest, m_parts[:, :, :, 1, :],
                                      ALU.subtract).then_inc(s_msp, 1)
                elif name == "stack_max":
                    dve.wait_ge(s_mTp, upto(l, b, ONE, 1))
                    dve.tensor_copy(mT[:], side[:].bitcast(BF16)[0:MROWS, 0:SEQ]).then_inc(s_mT, 1)
                    if l == 1 and isinstance(b, int) and b == 0:
                        dve.memset(probs[:], 0.0).then_inc(s_winz, 1)
                elif name == "pv" and l == 0 and n % T == T - 1:
                    g = n // T
                    dve.wait_ge(s_pv, upto(l, b, N_EXP, T * (g + 1)))
                    dve.tensor_copy(oT[:, g, :], side[:]).then_inc(s_oT, 1)
                elif name == "pv" and l == 1:
                    dve.wait_ge(s_pv, upto(l, b, N_EXP, n + 1))
                    dve.tensor_copy(oT[:, :, P * n:P * n + P],
                                    side[:].rearrange("p (g s) -> p g s", g=GROUPS)).then_inc(s_oT, 1)
                elif name == "out_T":
                    if not last(l, b):
                        dve.wait_ge(s_qw, upto(l, b, DMA2, 64))
                        dve.wait_ge(s_kw, upto(l, b, DMA2, 64))
                    for t in range(T):
                        o = wide[t // 2][:, t % 2, :].rearrange("p (h c) -> p h c", c=COL)
                        dve.wait_ge(s_o, upto(l, b, FOUR, t + 1))
                        dve.reciprocal(rden[:, t, :], o[:, :, HD]).then_inc(s_rden, 1)
                        dve.wait_ge(s_rden, upto(l, b, FOUR, t + 1))
                        dve.tensor_tensor(att[:, t, :].rearrange("p (h d) -> p h d", d=HD), o[:, :, 0:HD],
                                          rden[:, t, :].unsqueeze(2).to_broadcast([P, HEADS, HD]),
                                          ALU.mult).then_inc(s_att, 1)
                elif name == "project":
                    dve.wait_ge(s_pr, upto(l, b, ONE, 1))
                    dve.tensor_tensor(gated_a, wide[0][:, 0, :].rearrange("p (t d) -> p t d", t=T),
                                      gate_of(l, b, 0).to_broadcast([P, T, D]), ALU.mult).then_inc(s_gx, 1)
                    dve.wait_ge(s_gx, upto(l, b, ONE, 1))
                    dve.wait_ge(s_gbo, upto(l, b, ONE, 1))
                    dve.tensor_tensor(x_of(b), x_of(b), gated_a, ALU.add).then_inc(s_xa, 1)

            def experts(name, n, l, b):
                if name == "norm":
                    wait_apart(dve, s_xa, upto(l, b, ONE, 1))
                    for t in range(T):
                        dve.bn_stats(stats_f[:, t, :], x_tile(b, t)).then_inc(f_stat, 1)
                    normalise(l, b, stats_f, mv_f, rstd_f, xh_f, f_stat, f_aggr)
                elif name == "norm_T":
                    wait_apart(dve, f_rstd, upto(l, b, ONE, 1))
                    for t in range(T):
                        dve.tensor_scalar(xh_f[:, t, :], x_tile(b, t), mv_f[:, t, 0:1], rstd_f[:, t:t + 1],
                                          ALU.subtract, ALU.mult).then_inc(f_xh, 1)
                elif name == "logits":
                    dve.wait_ge(f_lg, upto(l, b, ONE, 1))
                    lg = side[:, 0:T * E].rearrange("p (t e) -> p t e", e=E)
                    if l == 0:
                        dve.tensor_tensor(logit[:], lg, ebias_sb[:].unsqueeze(1).to_broadcast([P, T, E]),
                                          ALU.add).then_inc(f_lb, 1)
                    else:
                        dve.tensor_copy(logit[:], lg).then_inc(f_lb, 1)
                    wait_apart(dve, f_lb, upto(l, b, ONE, 1))
                    for t in range(T):
                        dve.max(top[:, t, :], logit[:, t, :]).then_inc(f_m8, 1)
                    dve.wait_ge(f_m8, upto(l, b, FOUR, 4))
                    dve.tensor_tensor(gap[:], top[:, :, 1], top[:, :, 0], ALU.subtract).then_inc(f_gap, 1)
                    for t in range(T):
                        dve.max_index(top_i[:, t, :], top[:, t, :], logit[:, t, :]).then_inc(f_ix, 1)
                    dve.wait_ge(f_ix, upto(l, b, FOUR, 4))
                    dve.tensor_copy(top_if[:], top_i[:, :, 0:2]).then_inc(f_if, 1)
                elif name == "route":
                    dve.wait_ge(f_ge, upto(l, b, ONE, 1))
                    dve.tensor_scalar(gap_s[:], gap_e[:], 1.0, 2.0, ALU.add, ALU.mult).then_inc(f_w12, 1)
                    dve.wait_ge(f_w12, upto(l, b, THREE, 1))
                    dve.reciprocal(w_top[:, 0, :], gap_s[:]).then_inc(f_w12, 1)
                    dve.wait_ge(f_w12, upto(l, b, THREE, 2))
                    dve.tensor_tensor(w_top[:, 1, :], w_top[:, 0, :], gap_e[:], ALU.mult).then_inc(f_w12, 1)
                    dve.wait_ge(f_if, upto(l, b, ONE, 1))
                    dve.wait_ge(f_w12, upto(l, b, THREE, 3))
                    for k in range(2):
                        for t in range(T):
                            dve.tensor_scalar(pick[:, k, t, :], iota_f[:], top_if[:, t, k:k + 1],
                                              w_top[:, k, t:t + 1], ALU.is_equal, ALU.mult).then_inc(f_pick, 1)
                    dve.wait_ge(f_pick, upto(l, b, EIGHT, 8))
                    dve.tensor_tensor(cw[:], pick[:, 0, :, :], pick[:, 1, :, :], ALU.add).then_inc(f_cw, 1)
                elif name == "route_T":
                    dve.wait_ge(f_cwp, upto(l, b, ONE, 1))
                    dve.tensor_copy(cwT[:], side[0:E, :]).then_inc(f_cwT, 1)
                elif name == "split_h":
                    wait_apart(dve, f_hT, upto(l, b, ONE, 1))
                    dve.tensor_copy(h_hi[:], hT_f[:]).then_inc(f_hhi, 1)
                elif name == "unit":
                    if n < UNITS[l]:
                        dve.wait_ge(f_th, upto(l, b, UNITS, n + 1))
                        dve.scalar_tensor_tensor(out=silu[:, n % 2, :], in0=silu[:, n % 2, :], scalar=1.0,
                                                 in1=g_tile(l, b, n), op0=ALU.add, op1=ALU.mult).then_inc(f_sg, 1)
                        if n >= 2 and routed(l, n - 2):
                            dve.wait_ge(f_hw, upto(l, b, N_ROUTED, n - 1 - (HC if l == 0 else 0)))
                        elif n >= 2:
                            wait_split(dve, l, b, n - 2)
                        dve.wait_ge(f_u, upto(l, b, UNITS, n + 1))
                        dve.wait_ge(f_sg, upto(l, b, UNITS, n + 1))
                        if routed(l, n):
                            dve.tensor_tensor(hid[:, n % 2, :], silu[:, n % 2, :], u_ps[:],
                                              ALU.mult).then_inc(f_hid, 1)
                        else:
                            dve.scalar_tensor_tensor(out=hid[:, n % 2, :], in0=silu[:, n % 2, :], scalar=0.5,
                                                     in1=u_ps[:], op0=ALU.mult, op1=ALU.mult).then_inc(f_hid, 1)
                    i = n - 1
                    if 0 <= i < UNITS[l] and not early(l, b, i):
                        if last(l, b):
                            dve.wait_ge(f_hi, upto(l, b, N_EARLY, i + 1))
                            src = (hid_w if routed(l, i) else hid)[:, i % 2, :]
                        else:
                            src = before_hi(dve, l, b, i)
                            dve.tensor_copy(hid_hi[:, i % (LAG + 1), :], src).then_inc(f_hiv, 1)
                            dve.wait_ge(f_hiv, late_count(l, b, i))
                        dve.tensor_tensor(hid_lo[:, i % (LAG + 1), :], src, hid_hi[:, i % (LAG + 1), :].bitcast(F32),
                                          ALU.subtract).then_inc(f_lov, 1)
                elif name == "out":
                    dve.wait_ge(f_y, upto(l, b, ONE, 1))
                    dve.tensor_tensor(gated_f, g_ps[:].rearrange("p (t d) -> p t d", t=T),
                                      gate_of(l, b, 1).to_broadcast([P, T, D]), ALU.mult).then_inc(f_gy, 1)
                    wait_apart(dve, f_gy, upto(l, b, ONE, 1))
                    dve.tensor_tensor(x_of(b), x_of(b), gated_f, ALU.add).then_inc(f_xe, 1)

            def weights(name, n, second):
                pass

            run(dve, {"A": attention, "N": start, "R": experts, "F": experts, "W": weights})

        @block.tensor
        def _(pe):
            pe.wait_ge(s_cact, 1)
            for l in range(LAYERS):
                for w_ in range(2):
                    for k in range(2):
                        c0 = ((l * 2 + w_) * 2 + k) * B
                        mm = pe.matmul(wide[0][:, 0, c0:c0 + B], wmod_sb[:, l, 3 * w_ + k, :], c_act[:, l, :],
                                       start=True, stop=True)
            mm.then_inc(s_modps, 1)
            for l in range(LAYERS):
                for w_ in range(2):
                    mm = pe.matmul(wide[1][0:B, 0, D * (2 * l + w_):D * (2 * l + w_) + D], c_act[:, l, :],
                                   wmod_sb[:, l, 3 * w_ + 2, :], start=True, stop=True)
            mm.then_inc(s_gps, 1)
            pe.wait_ge(s_const, N_CONST)
            pe.wait_ge(s_identb, 1)
            pe.wait_ge(s_w, N_W)

            def scores(l, b, n):
                g, kt = n // T, KEY_TILES[n % T]
                lo, hi = (P * k for k in NEAR[kt])
                for two in range(2):
                    if n:
                        pe.wait_ge(s_ex, upto(l, b, N_EX, 2 * n + two - 1))
                    for half in range(2):
                        mm = pe.matmul(wide[two][:, half, lo:hi], ks[:, half, 2 * g + two, P * kt:P * kt + P],
                                       qs[:, 2 * g + two, lo:hi], start=True, stop=True)
                    mm.then_inc(s_T, 1)

            def times_v(l, b, n):
                g, i = n // T, n % T
                kt = KEY_TILES[i]
                lo, hi = (P * k for k in NEAR[kt])
                pe.wait_ge(s_cut, upto(l, b, [N_EXP[0], 0], n + 1))
                if i == 0 and g:
                    pe.wait_ge(s_oT, upto(l, b, FOUR, g))
                for j in range(4):
                    mm = pe.matmul(side[COL * j:COL * j + COL, lo:hi], V[:, kt, 4 * g + j, :],
                                   prob[:, n % 2, j, lo:hi], start=(i == 0), stop=True, skip_group_check=True)
                mm.then_inc(s_pv, 1)

            def window_scores(n, left, right):
                for h in range(HEADS):
                    pair, half = h // 2, h % 2
                    for w_ in range(2):
                        r, c0 = WIN * w_, P * n + WIN * w_
                        both = {"q": qs[:, pair, c0:c0 + WIN], "k": ks[:, half, pair, c0:c0 + WIN]}
                        mm = pe.matmul(wide[n % 2][r:r + WIN, h // 8, WIN * (h % 8):WIN * (h % 8) + WIN],
                                       both[left], both[right], start=True, stop=True)
                return mm

            def window_times_v(l, b, n):
                pe.wait_ge(s_ex, upto(l, b, N_EX, 2 * (n + 1)))
                if n:
                    pe.wait_ge(s_oT, upto(l, b, FOUR, n))
                for g in range(GROUPS):
                    for j in range(4):
                        mm = pe.matmul(side[COL * j:COL * j + COL, P * g:P * g + P], V[:, n, 4 * g + j, :],
                                       win_prob[:, n % 2, 4 * g + j, :], start=True, stop=True)
                mm.then_inc(s_pv, 1)

            def start(name, n, l, b):
                if name == "norm_T":
                    for t in range(T):
                        pe.wait_ge(s_xh, upto(l, b, FOUR, t + 1))
                        mm = pe.transpose(xT_ps[:, P * t:P * t + P], xh_a[:, t, :], ident[:])
                    mm.then_inc(s_xT, 1)
                elif name == "q":
                    pe.wait_ge(s_hT, upto(l, b, ONE, 1))
                    pe.matmul(wide[0][:, 0, :], wq_sb[l][:], hT_a[:], start=True, stop=True).then_inc(s_qps, 1)
                elif name == "k":
                    pe.matmul(wide[0][:, 1, :], wk_sb[l][:], hT_a[:], start=True, stop=True).then_inc(s_kps, 1)
                elif name == "v":
                    for t in range(T):
                        mm = pe.matmul(wide[1][:, 0, P * t:P * t + P], hT_a[:, P * t:P * t + P], wv_sb[l][:],
                                       start=True, stop=True)
                    mm.then_inc(s_vps, 1)

            def attention(name, n, l, b):
                if name == "max":
                    if n == 0:
                        if not first(l, b):
                            pe.wait_ge(s_gx, before(l, b, ONE))
                        pe.wait_ge(s_ones, 64)
                        pe.wait_ge(s_qs, upto(l, b, DMA_Q, 128))
                        pe.wait_ge(s_ks, upto(l, b, DMA_K, 96))
                        pe.wait_ge(s_v, upto(l, b, ONE, 1))
                    if n >= 2:
                        pe.wait_ge(s_mx, upto(l, b, N_MAX, n - 1))
                    if l == 1:
                        window_scores(n, "q", "k").then_inc(s_S, 1)
                        return
                    t, pair = n // PAIRS, n % PAIRS
                    lo, hi = (P * k for k in NEAR[t])
                    k0 = P * CUT[t]
                    for half in range(2):
                        pe.matmul(wide[n % 2][:, half, lo:hi], qs[:, pair, P * t:P * t + P],
                                  ks[:, half, pair, lo:hi], start=True, stop=True)
                    for half in range(2):
                        mm = pe.matmul(wide[n % 2][:, half, k0:k0 + P], ident_b[:],
                                       (cut_late if CUT[t] > t else cut_early)[:],
                                       start=False, stop=True, skip_group_check=True)
                    mm.then_inc(s_S, 1)
                elif name == "max_T":
                    if not first(l, b):
                        wait_apart(pe, f_cwT, before(l, b, ONE))
                    wait_apart(pe, s_msp, upto(l, b, FOUR, 4))
                    mT_ps = side[:].bitcast(BF16)
                    for t in range(T):
                        mm = pe.transpose(mT_ps[0:MROWS, P * t:P * t + P],
                                          m_parts[:, t].rearrange("p h c a -> p (h c a)"), ident_b[:])
                    mm.then_inc(s_mTp, 1)
                elif name == "exp":
                    if n == 0:
                        pe.wait_ge(s_mr, upto(l, b, DMA2, 32))
                        if not last(l, b):
                            pe.wait_ge(s_kf, upto(l, b, ONE, 2))
                    if l == 0:
                        scores(l, b, n)
                    else:
                        if n >= 2:
                            pe.wait_ge(s_ex, upto(l, b, N_EX, 2 * (n - 1)))
                        window_scores(n, "k", "q").then_inc(s_T, 1)
                elif name == "pv":
                    (times_v if l == 0 else window_times_v)(l, b, n)
                elif name == "out_T":
                    pe.wait_ge(s_oT, upto(l, b, FOUR, 4))
                    for t in range(T):
                        for g in range(GROUPS):
                            mm = pe.transpose(wide[t // 2][:, t % 2, P * g:P * g + P],
                                              oT[:, g, P * t:P * t + P], ident[:])
                        mm.then_inc(s_o, 1)
                elif name == "att_T":
                    for t in range(T):
                        pe.wait_ge(s_att, upto(l, b, FOUR, t + 1))
                        mm = pe.transpose(side[:, P * t:P * t + P], att[:, t, :], ident[:])
                    mm.then_inc(s_aTp, 1)
                elif name == "project":
                    pe.wait_ge(s_aT, upto(l, b, ONE, 1))
                    for t in range(T):
                        mm = pe.matmul(wide[0][:, 0, P * t:P * t + P], attT[:, P * t:P * t + P], wo_sb[l][:],
                                       start=True, stop=True)
                    mm.then_inc(s_pr, 1)

            def three_products(out_ps, w_at, r_hi, r_lo, start, stop):
                e, c0 = w_at
                pe.matmul(out_ps, w_hi[:, e, c0:c0 + P], r_hi, start=start, stop=False)
                pe.matmul(out_ps, w_hi[:, e, c0:c0 + P], r_lo, start=False, stop=False)
                return pe.matmul(out_ps, w_lo[:, e, c0:c0 + P], r_hi, start=False, stop=stop)

            def experts(name, n, l, b):
                if name == "norm_T":
                    for t in range(T):
                        pe.wait_ge(f_xh, upto(l, b, FOUR, t + 1))
                        mm = pe.transpose(side[:, P * t:P * t + P], xh_f[:, t, :], ident[:])
                    mm.then_inc(f_xT, 1)
                elif name == "logits":
                    pe.wait_ge(f_hT, upto(l, b, ONE, 1))
                    for t in range(T):
                        mm = pe.matmul(side[:, E * t:E * t + E], hT_f[:, P * t:P * t + P], router_sb[l][:],
                                       start=True, stop=True)
                    mm.then_inc(f_lg, 1)
                elif name == "route_T":
                    pe.wait_ge(f_cw, upto(l, b, ONE, 1))
                    for t in range(T):
                        mm = pe.transpose(side[0:E, P * t:P * t + P], cw[:, t, :], ident[:])
                    mm.then_inc(f_cwp, 1)
                elif name == "unit":
                    if n < UNITS[l]:
                        e, c = expert_of(l, n), n % HC
                        if n == 0:
                            pe.wait_ge(f_hlo, upto(l, b, ONE, 1))
                        elif not last(l, b):
                            pe.wait_ge(f_sg, upto(l, b, UNITS, n))
                        elif n >= 2:
                            pe.wait_ge(f_sg, upto(l, b, UNITS, n - 1))
                        if c == 0:
                            pe.wait_ge(s_wlo, n // HC + 1 + l * EXPERTS[0])
                        three_products(g_tile(l, b, n), (e, P * c), h_hi[:], h_lo[:], True, True).then_inc(f_g, 1)
                        if n:
                            pe.wait_ge(f_hid, upto(l, b, UNITS, n))
                        three_products(u_ps[:], (e, HID + P * c), h_hi[:], h_lo[:], True, True).then_inc(f_u, 1)
                    i = n - LAG
                    if 0 <= i < UNITS[l]:
                        e, c = expert_of(l, i), i % HC
                        wait_split(pe, l, b, i)
                        three_products(y_ps[:], (e, UP + D * c), hid_hi[:, i % (LAG + 1), :], hid_lo[:, i % (LAG + 1), :],
                                       i == 0, i == UNITS[l] - 1).then_inc(f_dn, 1)
                elif name == "out_T":
                    pe.wait_ge(f_yT, upto(l, b, ONE, 1))
                    for t in range(T):
                        mm = pe.transpose(g_ps[:, P * t:P * t + P], yT[:, P * t:P * t + P], ident[:])
                    mm.then_inc(f_y, 1)

            def weights(name, n, second):
                pass

            run(pe, {"A": attention, "N": start, "R": experts, "F": experts, "W": weights})


def build(nc, arrays):
    aps = {n: nc.dram_tensor(n, a.shape, F32, kind="ExternalInput").ap() for n, a in arrays.items()}
    out = nc.dram_tensor("out", (B, SEQ, D), F32, kind="ExternalOutput").ap()
    two = {n: [aps[f"{n}{l}"] for l in range(LAYERS)]
           for n in ("cT", "wmod", "wq", "wk", "wv", "wo", "bq", "bk", "bv", "bo", "router", "wexp")}
    adaln_two_layers(nc, aps["x"], two["cT"], two["wmod"], two["wq"], two["wk"], two["wv"], two["wo"],
                     two["bq"], two["bk"], two["bv"], two["bo"], two["router"], aps["ebias"],
                     two["wexp"], out)


def layout(inputs):
    import numpy as np

    a = {n: np.asarray(v) for n, v in inputs.items()}

    def by_half(w):
        return w.reshape(-1, PAIRS, 2, HD).transpose(0, 2, 3, 1).reshape(-1, D)

    def experts(ups, gates, downs):
        g, u, d = (np.concatenate(ws, 0) for ws in (ups, gates, downs))
        d = d.reshape(-1, HC, P, D).transpose(2, 0, 1, 3).reshape(P, -1, DOWN)
        return np.concatenate([g.transpose(1, 0, 2), u.transpose(1, 0, 2), d], 2).reshape(P, -1)

    qkv, bqkv = a["L1_attn_w_qkv"], a["L1_attn_b_qkv"]
    got = {
        "x": a["L0_attn_hidden_states"],
        "cT0": a["L0_c"].T, "cT1": a["L1_c"].T, "wmod0": a["L0_wmod"], "wmod1": a["L1_wmod"],
        "wq0": by_half(a["L0_attn_wq"]), "wk0": by_half(a["L0_attn_wk"]),
        "wv0": a["L0_attn_wv"], "wo0": a["L0_attn_wo"],
        "bq0": by_half(a["L0_attn_bq"][None]).T, "bk0": by_half(a["L0_attn_bk"][None]).T,
        "bv0": a["L0_attn_bv"], "bo0": a["L0_attn_bo"],
        "wq1": by_half(qkv[:, 0:D]), "wk1": by_half(qkv[:, D:2 * D]), "wv1": qkv[:, 2 * D:],
        "wo1": a["L1_attn_w_out"],
        "bq1": by_half(bqkv[None, 0:D]).T, "bk1": by_half(bqkv[None, D:2 * D]).T, "bv1": bqkv[2 * D:],
        "bo1": a["L1_attn_b_out"],
        "router0": a["L0_ffn_router_w"].T, "router1": a["L1_ffn_gate_kernel"],
        "ebias": a["L0_ffn_experts_bias"],
        "wexp0": experts((a["L0_ffn_w1"], a["L0_ffn_sw1"]), (a["L0_ffn_w3"], a["L0_ffn_sw3"]),
                         (a["L0_ffn_w2"], a["L0_ffn_sw2"])),
        "wexp1": experts((a["L1_ffn_w0_kernel"],), (a["L1_ffn_w1_kernel"],), (a["L1_ffn_wo_kernel"],)),
    }
    return {n: np.ascontiguousarray(v) for n, v in got.items()}


def kernel(**inputs):
    import concourse.bacc as bacc
    from concourse.bass_utils import run_bass_kernel_spmd

    nc = bacc.Bacc("TRN2", target_bir_lowering=False, num_devices=1)
    arrays = layout(inputs)
    build(nc, arrays)
    r = run_bass_kernel_spmd(nc, [arrays], core_ids=[0])
    return r.results[0]["out"]
```
